# Optimizing a Trainium2 kernel written in Bass

```python
import numpy as np
import jax
import jax.numpy as jnp

def _softmax(x, axis=-1):
    return jax.nn.softmax(x, axis=axis)

def _gelu(x):
    return jax.nn.gelu(x, approximate=True)

def _silu(x):
    return jax.nn.silu(x)

def _sigmoid(x):
    return jax.nn.sigmoid(x)

def _layernorm(x, axis=-1, eps=1e-05):
    m = jnp.mean(x, axis=axis, keepdims=True)
    v = jnp.var(x, axis=axis, keepdims=True)
    return (x - m) / jnp.sqrt(v + eps)

def _scatter_add(tgt, idx, src, axis=0):
    return tgt.at[idx].add(src)

def _segment_sum(src, seg, n):
    return jax.ops.segment_sum(src, seg, n)
kernel_name = 'mk_seq_preln_d1_jaxref_r4_37a8a3'

def setup_inputs(seed: int=0):
    np.random.seed(seed)
    _w = jnp.asarray

    def _L0_attn_setup():
        import jax, jax.numpy as jnp
        import numpy as np
        B, N, C, H = (4, 2048, 256, 16)
        D = C // H
        EPS = 1e-05
        key = jax.random.key(seed)
        ks = jax.random.split(key, 10)
        s = 1.0 / np.sqrt(C)
        return {'x': jax.random.normal(ks[0], (B, N, C), jnp.float32), 'Wq': jax.random.uniform(ks[1], (C, C), jnp.float32, -s, s), 'bq': jax.random.uniform(ks[2], (C,), jnp.float32, -s, s), 'Wk': jax.random.uniform(ks[3], (C, C), jnp.float32, -s, s), 'bk': jax.random.uniform(ks[4], (C,), jnp.float32, -s, s), 'Wv': jax.random.uniform(ks[5], (C, C), jnp.float32, -s, s), 'bv': jax.random.uniform(ks[6], (C,), jnp.float32, -s, s), 'Wo': jax.random.uniform(ks[7], (C, C), jnp.float32, -s, s), 'bo': jax.random.uniform(ks[8], (C,), jnp.float32, -s, s), 'ln_g': jnp.ones((C,), jnp.float32), 'ln_b': jnp.zeros((C,), jnp.float32)}
    _L0_attn_in = _L0_attn_setup()

    def _L0_ffn_setup():
        import jax, jax.numpy as jnp
        import numpy as np
        DIM = 256
        N_EXPERTS = 16
        TOP_K = 4
        N_GROUP = 4
        TOPK_GROUP = 2
        MOE_INTER = 128
        SHARED_INTER = 512
        ROUTED_SCALE = 2.5

        def relu2(x):
            return jnp.square(jax.nn.relu(x))

        def _router(x2, gate_w, bias_e):
            T = x2.shape[0]
            logits = x2 @ gate_w.T
            scores = jax.nn.sigmoid(logits)
            sc = jax.lax.stop_gradient(scores + bias_e[None, :])
            grp = sc.reshape(T, N_GROUP, N_EXPERTS // N_GROUP)
            top2, _ = jax.lax.top_k(grp, 2)
            group_scores = top2.sum(-1)
            _, gidx = jax.lax.top_k(group_scores, TOPK_GROUP)
            rows = jnp.arange(T)[:, None]
            gmask = jnp.zeros((T, N_GROUP), dtype=sc.dtype).at[rows, gidx].set(1.0)
            smask = jnp.repeat(gmask, N_EXPERTS // N_GROUP, axis=1)
            masked = jnp.where(smask > 0, sc, 0.0)
            _, topk_idx = jax.lax.top_k(masked, TOP_K)
            topk_w = jnp.take_along_axis(scores, topk_idx, axis=1)
            topk_w = topk_w / (topk_w.sum(-1, keepdims=True) + 1e-20)
            topk_w = topk_w * ROUTED_SCALE
            return (topk_idx, topk_w)
        key = jax.random.key(seed)
        ks = jax.random.split(key, 6)
        hidden_states = jax.random.normal(ks[0], (2, 512, DIM), dtype=jnp.float32)
        gate_w = jax.random.normal(ks[1], (N_EXPERTS, DIM), dtype=jnp.float32) * 0.02
        bias_e = jnp.zeros((N_EXPERTS,), dtype=jnp.float32)
        up_w = jax.random.normal(ks[2], (N_EXPERTS, MOE_INTER, DIM), dtype=jnp.float32) * 0.02
        down_w = jax.random.normal(ks[3], (N_EXPERTS, DIM, MOE_INTER), dtype=jnp.float32) * 0.02
        shared_up = jax.random.normal(ks[4], (SHARED_INTER, DIM), dtype=jnp.float32) * 0.02
        shared_down = jax.random.normal(ks[5], (DIM, SHARED_INTER), dtype=jnp.float32) * 0.02
        return {'hidden_states': hidden_states, 'gate_w': gate_w, 'bias_e': bias_e, 'up_w': up_w, 'down_w': down_w, 'shared_up': shared_up, 'shared_down': shared_down}
    _L0_ffn_in = _L0_ffn_setup()
    _d = {'L0_attn_x': _L0_attn_in['x'], 'L0_attn_Wq': _L0_attn_in['Wq'], 'L0_attn_bq': _L0_attn_in['bq'], 'L0_attn_Wk': _L0_attn_in['Wk'], 'L0_attn_bk': _L0_attn_in['bk'], 'L0_attn_Wv': _L0_attn_in['Wv'], 'L0_attn_bv': _L0_attn_in['bv'], 'L0_attn_Wo': _L0_attn_in['Wo'], 'L0_attn_bo': _L0_attn_in['bo'], 'L0_attn_ln_g': _L0_attn_in['ln_g'], 'L0_attn_ln_b': _L0_attn_in['ln_b'], 'L0_ffn_gate_w': _L0_ffn_in['gate_w'], 'L0_ffn_bias_e': _L0_ffn_in['bias_e'], 'L0_ffn_up_w': _L0_ffn_in['up_w'], 'L0_ffn_down_w': _L0_ffn_in['down_w'], 'L0_ffn_shared_up': _L0_ffn_in['shared_up'], 'L0_ffn_shared_down': _L0_ffn_in['shared_down']}
    _x0 = _d['L0_attn_x']
    _d['L0_attn_x'] = jax.random.normal(jax.random.fold_in(jax.random.key(seed), 1), (4, 1024, 256), dtype=_x0.dtype)
    del _x0
    return _d

def reference(L0_attn_x, L0_attn_Wq, L0_attn_bq, L0_attn_Wk, L0_attn_bk, L0_attn_Wv, L0_attn_bv, L0_attn_Wo, L0_attn_bo, L0_attn_ln_g, L0_attn_ln_b, L0_ffn_gate_w, L0_ffn_bias_e, L0_ffn_up_w, L0_ffn_down_w, L0_ffn_shared_up, L0_ffn_shared_down):

    def _L0_attn_ref(x, Wq, bq, Wk, bk, Wv, bv, Wo, bo, ln_g, ln_b):
        import jax, jax.numpy as jnp
        import numpy as np
        B, N, C, H = (4, 2048, 256, 16)
        D = C // H
        EPS = 1e-05
        b, n, c = x.shape
        q = x @ Wq.T + bq
        k = x @ Wk.T + bk
        v = x @ Wv.T + bv
        split = lambda z: z.reshape(b, n, H, D).transpose(0, 2, 1, 3)
        q, k, v = (split(q), split(k), split(v))
        q = jax.nn.softmax(q, axis=-1)
        k = jax.nn.softmax(k, axis=-2)
        state = jnp.einsum('bhnd,bhne->bhde', k, v)
        out = jnp.einsum('bhnd,bhde->bhne', q, state)
        out = out.transpose(0, 2, 1, 3).reshape(b, n, c)
        mu = out.mean(-1, keepdims=True)
        var = out.var(-1, keepdims=True)
        out = (out - mu) * jax.lax.rsqrt(var + EPS) * ln_g + ln_b
        return out @ Wo.T + bo

    def _L0_ffn_ref(hidden_states, gate_w, bias_e, up_w, down_w, shared_up, shared_down):
        import jax, jax.numpy as jnp
        import numpy as np
        DIM = 256
        N_EXPERTS = 16
        TOP_K = 4
        N_GROUP = 4
        TOPK_GROUP = 2
        MOE_INTER = 128
        SHARED_INTER = 512
        ROUTED_SCALE = 2.5

        def relu2(x):
            return jnp.square(jax.nn.relu(x))

        def _router(x2, gate_w, bias_e):
            T = x2.shape[0]
            logits = x2 @ gate_w.T
            scores = jax.nn.sigmoid(logits)
            sc = jax.lax.stop_gradient(scores + bias_e[None, :])
            grp = sc.reshape(T, N_GROUP, N_EXPERTS // N_GROUP)
            top2, _ = jax.lax.top_k(grp, 2)
            group_scores = top2.sum(-1)
            _, gidx = jax.lax.top_k(group_scores, TOPK_GROUP)
            rows = jnp.arange(T)[:, None]
            gmask = jnp.zeros((T, N_GROUP), dtype=sc.dtype).at[rows, gidx].set(1.0)
            smask = jnp.repeat(gmask, N_EXPERTS // N_GROUP, axis=1)
            masked = jnp.where(smask > 0, sc, 0.0)
            _, topk_idx = jax.lax.top_k(masked, TOP_K)
            topk_w = jnp.take_along_axis(scores, topk_idx, axis=1)
            topk_w = topk_w / (topk_w.sum(-1, keepdims=True) + 1e-20)
            topk_w = topk_w * ROUTED_SCALE
            return (topk_idx, topk_w)
        B, S, D = hidden_states.shape
        x2 = hidden_states.reshape(-1, D)
        T = x2.shape[0]
        topk_idx, topk_w = _router(x2, gate_w, bias_e)
        rows = jnp.arange(T)[:, None]
        combine = jnp.zeros((T, N_EXPERTS), dtype=topk_w.dtype).at[rows, topk_idx].add(topk_w)

        def body(acc, inp):
            wu, wd, cw = inp
            y = relu2(x2 @ wu.T) @ wd.T
            return (acc + cw[:, None] * y, None)
        routed, _ = jax.lax.scan(body, jnp.zeros_like(x2), (up_w, down_w, combine.T))
        shared = relu2(x2 @ shared_up.T) @ shared_down.T
        out = routed + shared
        return out.reshape(B, S, D)
    x = L0_attn_x
    x = x + _L0_attn_ref(_layernorm(x, axis=-1), L0_attn_Wq, L0_attn_bq, L0_attn_Wk, L0_attn_bk, L0_attn_Wv, L0_attn_bv, L0_attn_Wo, L0_attn_bo, L0_attn_ln_g, L0_attn_ln_b)
    x = x + _L0_ffn_ref(_layernorm(x, axis=-1), L0_ffn_gate_w, L0_ffn_bias_e, L0_ffn_up_w, L0_ffn_down_w, L0_ffn_shared_up, L0_ffn_shared_down)
    return x

_drawn_inputs = setup_inputs


def setup_inputs(seed=0):
    import zlib

    import numpy as np

    out = dict(_drawn_inputs(seed))
    spreads = {'L0_attn_ln_g': (1.0, 0.2), 'L0_attn_ln_b': (0.0, 0.1), 'L0_ffn_bias_e': (0.0, 0.316)}
    factors = {'L0_attn_bq': 8.0, 'L0_attn_bk': 8.0}
    for name, (base, spread) in spreads.items():
        noise = np.random.default_rng([zlib.crc32(name.encode()), seed]).standard_normal(out[name].shape)
        drawn = base * np.exp(spread * noise) if base else spread * noise
        out[name] = jnp.asarray(drawn.astype(out[name].dtype))
    for name, factor in factors.items():
        out[name] = (out[name] * factor).astype(out[name].dtype)
    return out
```

```python
from contextlib import ExitStack

import concourse.bass as bass
from concourse import mybir

F32 = mybir.dt.float32
F32R = mybir.dt.float32r
ALU = mybir.AluOpType
ACT = mybir.ActivationFunctionType
AX = mybir.AxisListType

P = 128
EPS = 1e-5
TPG = 4
GT = TPG * P
BANK = 512
LAG = 2
WCHUNK = 512
STAGE = 4

FILLS = {
    "xT": (0, 1), "k": (2, 3), "qv01": (0, 1), "qv23": (2, 3), "qT": (0, 1),
    "eT0": (0,), "eT1": (1,), "eT2": (0,), "eT3": (1,), "st3": (2, 3),
    "out": (0, 1), "oT": (2, 3), "wo": (0, 1), "fT": (2, 3), "gate": (0,), "gT": (1,),
    "ffn_out": (2, 3),
}
SIGNALS = {
    "ln_x_stats": 3, "ln_o_stats": 3, "ln_f_stats": 3,
    "ln_x_root": 2, "ln_o_root": 2, "ln_f_root": 2,
    "ln_x_apply": 4, "ln_o_apply": 3, "ln_f_apply": 4,
    "xT_hi": 2, "oT_hi": 2, "fT_hi": 2,
    "oT_lo": 2, "k_top": 2, "softmax_max": 1,
    "softmax_sub": 1, "softmax_mul": 1, "residual": 1,
    "softmax_exp": 1, "k_exp": 2,
    "softmax_sum": 2, "k_max": 2, "k_sum": 1,
    "st_part": 2,
    "route_pick": 25, "route_weight": 4,
    "route_root": 2,
}
ONCE_A_SEQUENCE = {"k_exp", "k_max", "k_sum", "st_part"}

PROLOGUE = (
    [(s, 0) for s in ("ln_x_stats", "ln_x_root", "ln_x_apply", "xT", "k", "qv01", "qv23", "softmax_max",
                      "softmax_sub")]
    + [(s, 1) for s in ("ln_x_stats", "ln_x_root", "ln_x_apply")]
    + [(s, 0) for s in ("softmax_exp", "softmax_sum", "softmax_mul")]
    + [(s, 1) for s in ("xT", "k")] + [("k_max", 0), ("k_exp", 0), ("qT", 0)]
    + [(s, 1) for s in ("qv01", "qv23", "softmax_max", "softmax_sub", "softmax_exp", "softmax_sum",
                        "softmax_mul", "qT")]
    + [(s, 0) for s in ("k_sum", "eT0", "eT1", "st0", "eT2", "st1", "eT3", "st2", "st3", "state", "residual",
                        "out", "ln_o_stats", "ln_o_root", "ln_o_apply", "oT", "wo",
                        "ln_f_stats", "ln_f_root", "ln_f_apply", "fT", "gate", "route_pick",
                        "route_root", "route_weight", "gT")]
)
SLOT_EVEN = {
    0: [("out", 1), ("ln_o_stats", 1), ("ln_o_root", 1), ("ln_x_stats", 2), ("ln_x_root", 2), ("residual", 1)],
    1: [("ln_o_apply", 1), ("ln_x_apply", 2)],
    3: [("oT", 1)],
    5: [("wo", 1), ("ln_f_stats", 1), ("ln_f_root", 1)],
    6: [("ln_f_apply", 1), ("xT", 2)],
    8: [("fT", 1), ("k", 2)],
    9: [("qv01", 2), ("ln_x_stats", 3), ("ln_x_root", 3)],
    10: [("qv23", 2), ("gate", 1), ("ln_x_apply", 3), ("softmax_max", 2), ("softmax_sub", 2)],
    11: [("route_pick", 1), ("route_root", 1)],
    12: [("route_weight", 1), ("xT", 3), ("softmax_exp", 2), ("softmax_sum", 2), ("softmax_mul", 2)],
    14: [("gT", 1), ("k", 3)],
    15: [("qT", 2)],
    17: [("qv01", 3)],
    18: [("qv23", 3)],
    19: [("softmax_max", 3), ("softmax_sub", 3)],
}
SLOT_ODD = {
    -1: [("ffn_evac", 0)],
    0: [("ffn_out", 0), ("k_max", 2), ("k_exp", 2)],
    1: [("k_sum", 2), ("softmax_exp", 3)],
    2: [("softmax_sum", 3), ("softmax_mul", 3)],
    4: [("qT", 3)],
    5: [("eT0", 2), ("eT1", 2)],
    7: [("st0", 2), ("eT2", 2)],
    8: [("st1", 2), ("eT3", 2)],
    9: [("st2", 2)],
    10: [("st3", 2), ("state", 2), ("residual", 2)],
    11: [("out", 2), ("ln_o_stats", 2), ("ln_o_root", 2)],
    12: [("ln_o_apply", 2)],
    13: [("oT", 2)],
    15: [("wo", 2), ("ln_f_stats", 2), ("ln_f_root", 2)],
    16: [("ln_f_apply", 2)],
    17: [("fT", 2)],
    19: [("gate", 2), ("route_pick", 2), ("route_root", 2)],
    20: [("route_weight", 2)],
    21: [("gT", 2)],
    22: [("ffn_evac", 1), ("ffn_out", 1)],
}


def without_next(slot):
    return {s: [x for x in steps if x[1] < 2] for s, steps in slot.items()}


def layer_kernel(nc, x, weights, rows, columns, masks, out):
    TOKENS, C = x.shape
    E, EG = 16, 4
    CH = weights.shape[1] // (2 * C) - 4
    KC = C // P
    HD = 16
    HEADS = C // HD
    GROUPS = TOKENS // GT
    SEQS = GROUPS // 2
    TPS = 2 * TPG
    ITER = SEQS - 1
    NW = weights.shape[1]
    NWC = NW // WCHUNK
    QKV0, WO0, UP0 = 0, KC * 3 * C, KC * 4 * C
    DOWN0 = UP0 + CH * C
    NONE = -3.0e38

    first_split = 4
    prologue = list(PROLOGUE[:first_split])
    split_at = UP0 // WCHUNK
    for n, entry in enumerate(PROLOGUE[first_split:]):
        prologue.append(entry)
        if n % 2 == 0 and split_at < NWC:
            prologue.append(("split", split_at))
            split_at += 1
    assert split_at == NWC

    def flat(i, even, odd):
        return [(n, g + 2 * i) for t in (even, odd) for s in sorted(t) for n, g in t[s]]

    order = list(prologue)
    for i in range(ITER):
        order += flat(i, SLOT_EVEN, SLOT_ODD)
    order += flat(ITER, without_next(SLOT_EVEN), without_next(SLOT_ODD))
    place = {x: n for n, x in enumerate(order)}

    def value(f, group):
        if isinstance(group, tuple):
            i, g = group
            step = f(g + 2) - f(g)
            return i * step + f(g) if step else f(g)
        return f(group)

    def shift(group, by):
        return (group[0], group[1] + by) if isinstance(group, tuple) else group + by

    def half(group):
        return (group[1] if isinstance(group, tuple) else group) % 2

    def ahead(step, group, bank):
        return value(lambda g: sum(FILLS.get(s, ()).count(bank) for s, _ in order[:place[step, g]]), group)

    def fill(step, j, group):
        bank = FILLS[step][j]
        return bank, ahead(step, group, bank) + FILLS[step][:j + 1].count(bank)

    def wait(eng, sem, v):
        if not isinstance(v, int) or v > 0:
            eng.wait_ge(sem, v)

    with ExitStack() as ctx:
        def sb(name, shape, dt=F32):
            return ctx.enter_context(nc.sbuf_tensor(name, shape, dt))

        def sem(name):
            return ctx.enter_context(nc.semaphore(name))

        w_hi = sb("w_hi", [P, NW], F32R)
        w_lo = sb("w_lo", [P, NW], F32R)
        x_tok = sb("x_tok", [P, TPG, C])
        q_tok = sb("q_tok", [P, TPG, C])
        v_tok = sb("v_tok", [P, TPS, C])
        n_tok = sb("n_tok", [P, TPG, C])
        act_hi = sb("act_hi", [P, KC, GT], F32R)
        act_lo = sb("act_lo", [P, KC, GT], F32R)
        k_chan = sb("k_chan", [P, KC, 2 * GT])
        q_chan = sb("q_chan", [P, KC, 2 * GT])
        o_chan = sb("o_chan", [P, KC, GT])
        x1 = sb("x1", [P, TPS, C])
        f_hi = sb("f_hi", [P, 2, KC, GT], F32R)
        f_lo = sb("f_lo", [P, 2, KC, GT], F32R)
        g_chan = sb("g_chan", [E, GT])
        g_rows = sb("g_rows", [P, EG, GT])
        GB, YB, HB = 2, 3, 2
        g_all = sb("g_all", [P, GB, GT])
        y = sb("y", [P, YB, GT])
        y_hi = sb("y_hi", [P, HB, GT], F32R)
        y_lo = sb("y_lo", [P, HB, GT], F32R)
        state = sb("state", [P, KC, P])
        row_c = sb("row_c", [P, rows.shape[0]])
        col_c = sb("col_c", [P, columns.shape[1]])
        mask_c = sb("mask_c", [P, masks.shape[1]])
        LN = ("x", "o", "f")
        stats = sb("stats", [P, 3, TPG, 6])
        mv = sb("mv", [P, 3, TPG, 2])
        root = sb("root", [P, 3, 4, TPG])
        qmax = sb("qmax", [P, TPG * HEADS])
        qsum = sb("qsum", [P, 2, TPG * HEADS])
        kmax = sb("kmax", [P, KC, 2])
        kneg = sb("kneg", [P, 2, KC])
        ksum = sb("ksum", [P, 2, KC])
        r_score = sb("r_score", [P, TPG, E])
        r_pick = sb("r_pick", [P, TPG, E])
        r_half = sb("r_half", [P, 2, TPG * EG, 2])
        r_pair = sb("r_pair", [P, TPG * EG, 3])
        r_group = sb("r_group", [P, 2, TPG, EG])
        r_above = sb("r_above", [P, 2, TPG * EG, EG])
        r_list = sb("r_list", [P, TPG, E + 4])
        r_best = sb("r_best", [P, TPG, 8])
        r_left = sb("r_left", [P, TPG, E + 4])
        r_sum = sb("r_sum", [P, 2, TPG])
        r_root = sb("r_root", [P, 4, TPG, E])

        b_qv, b_o, b_e = row_c[:, 0:2 * C], row_c[:, 2 * C:3 * C], row_c[:, 3 * C:3 * C + E]
        b_k, ln_g, ln_b = col_c[:, 0:KC], col_c[:, KC:2 * KC], col_c[:, 2 * KC:3 * KC]
        gate_w = col_c[:, 3 * KC:3 * KC + KC * E]
        ident, same_head, earlier = mask_c[:, 0:P], mask_c[:, P:2 * P], mask_c[:, 2 * P:2 * P + EG * EG]
        stage = g_rows

        hid = ctx.enter_context(nc.psum_tensor("hid", [P, 2, BANK], F32))
        down = ctx.enter_context(nc.psum_tensor("down", [P, KC, BANK], F32))
        att = ctx.enter_context(nc.psum_tensor("att", [P, 4, BANK], F32))

        consts_in = sem("consts_in")
        w_in = [sem(f"w_in{k}") for k in range(STAGE)]
        w_hi_done = sem("w_hi_done")
        w_lo_done = sem("w_lo_done")
        x_in = sem("x_in")
        res_in = [sem(f"res_in{k}") for k in range(2)]
        stored = [sem(f"stored{k}") for k in range(2)]
        bank_full = [sem(f"bank_full{k}") for k in range(4)]
        bank_read = [sem(f"bank_read{k}") for k in range(4)]
        signal = {s: sem(s) for s in SIGNALS}
        g_rows_in = sem("g_rows_in")
        g_all_done = sem("g_all_done")
        list_end = sem("list_end")
        hid_done = sem("hid_done")
        y_rooted = sem("y_rooted")
        y_squared = sem("y_squared")
        y_hi_done = sem("y_hi_done")
        y_lo_done = sem("y_lo_done")
        y_used = sem("y_used")
        down_read = sem("down_read")

        passed = {e: sem(f"passed_{e.name}") for e in (nc.sync.engine, nc.vector.engine, nc.gpsimd.engine)}

        def runs(step, group):
            per = SIGNALS[step]
            return value(lambda g: (g // 2 if step in ONCE_A_SEQUENCE else g) * per, group)

        def after(eng, step, group, k=None):
            eng.wait_ge(signal[step], runs(step, group) + (SIGNALS[step] if k is None else k))

        def filled(eng, step, j, group):
            bank, n = fill(step, j, group)
            eng.wait_ge(bank_full[bank], n)
            return att[:, bank, :]

        def read(eng, step, j, group):
            bank, n = fill(step, j, group)
            eng.wait_ge(bank_read[bank], n)

        def all_filled(eng, bank, step, group):
            wait(eng, bank_full[bank], ahead(step, group, bank))

        def reader_of(step, j):
            return bank_read[FILLS[step][j]]

        def credited(per_group, k, group):
            return value(lambda g: (g + 1) * per_group + k + 1, group)

        def counted(per_group, k, group):
            return value(lambda g: g * per_group + k + 1, group)

        def steps_at(slot, s, i, mine):
            for name, g in slot.get(s, ()):
                if name in mine:
                    mine[name](2 * i + g if isinstance(i, int) else (i, g))

        def stand_alone(eng):
            eng.sem_inc(passed[eng.engine], 1)

        block = ctx.enter_context(nc.Block())

        @block.sync
        def _(sp):
            def tokens(dram, group):
                first = value(lambda g: g * GT, group)
                return dram[bass.ds(first, GT), :].rearrange("(t p) c -> p t c", p=P)

            def half_of(group):
                return slice(half(group) * TPG, (half(group) + 1) * TPG)

            def load_x(group):
                if group != 0:
                    bank, n = fill("xT", KC - 1, shift(group, -1))
                    sp.wait_ge(bank_full[bank], n)
                    stand_alone(sp)
                sp.dma_start(x_tok[:], tokens(x, group)).then_inc(x_in, 16)

            def load_residual(group):
                wait(sp, stored[half(group)], value(lambda g: 16 * (g // 2), group))
                stand_alone(sp)
                sp.dma_start(x1[:, half_of(group), :], tokens(x, group)).then_inc(
                    res_in[half(group)], 16)

            def spread_rows(group):
                read(sp, "gT", 0, group)
                stand_alone(sp)
                wait(sp, g_all_done, value(lambda g: g * E, group))
                for r in range(E // EG):
                    sp.dma_start(g_rows[32 * r:32 * r + 1, :, :], g_chan[EG * r:EG * (r + 1), :]).then_inc(
                        g_rows_in, 16)

            def store(group):
                for j in range(2):
                    read(sp, "ffn_out", j, group)
                stand_alone(sp)
                sp.dma_start(tokens(out, group), x1[:, half_of(group), :]).then_inc(
                    stored[half(group)], 16)

            load_x(0)
            sp.dma_start(mask_c[:], masks).then_inc(consts_in, 16)
            sp.dma_start(row_c[:], rows.partition_broadcast(P)).then_inc(consts_in, 16)
            sp.dma_start(col_c[:], columns).then_inc(consts_in, 16)
            for c in range(NWC):
                if c >= STAGE:
                    sp.wait_ge(w_lo_done, c - STAGE + 1)
                sp.dma_start(stage[:, c % STAGE, :], weights[:, c * WCHUNK:(c + 1) * WCHUNK]).then_inc(
                    w_in[c % STAGE], 16)
                if c == UP0 // WCHUNK:
                    load_x(1)
            load_residual(0)
            load_residual(1)
            sp.wait_ge(w_lo_done, NWC)
            spread_rows(0)
            with sp.Fori(0, ITER) as i:
                load_x((i, 2))
                load_x((i, 3))
                spread_rows((i, 1))
                store((i, 0))
                load_residual((i, 2))
                spread_rows((i, 2))
                store((i, 1))
                load_residual((i, 3))
            spread_rows(GROUPS - 1)
            store(GROUPS - 2)
            store(GROUPS - 1)
            for k in range(2):
                sp.wait_ge(stored[k], 16 * SEQS)

        @block.tensor
        def _(pe):
            def take(step, j, group):
                bank, n = fill(step, j, group)
                wait(pe, bank_read[bank], n - 1)
                return att[:, bank, :], bank_full[bank]

            def product(dst, w_at, w_n, a_hi, a_lo, tokens_stationary):
                n = 0
                for w, a in ((w_hi, a_hi), (w_lo, a_hi), (w_hi, a_lo)):
                    for k in range(KC):
                        wk = w[:, w_at(k):w_at(k) + w_n]
                        lhs, rhs = (a(k), wk) if tokens_stationary else (wk, a(k))
                        mm = pe.matmul(dst, lhs, rhs, start=n == 0, stop=n == 3 * KC - 1)
                        n += 1
                return mm

            def turn(step, source, group):
                for c in range(KC):
                    dst, full = take(step, c, group)
                    for t in range(TPG):
                        mm = pe.transpose(dst[:, t * P:(t + 1) * P], source[:, t, c * P:(c + 1) * P], ident)
                    mm.then_inc(full, 1)

            def turn_back(step, j, source, at, group):
                dst, full = take(step, j, group)
                for t in range(2):
                    for c in range(KC):
                        mm = pe.transpose(dst[:, t * C + c * P:t * C + (c + 1) * P],
                                          source[:, c, at + t * P:at + (t + 1) * P], ident)
                mm.then_inc(full, 1)

            def x_turn(group):
                after(pe, "ln_x_apply", group)
                turn("xT", x_tok, group)

            def k_project(group):
                for c in range(KC):
                    read(pe, "xT", c, group)
                for c in range(KC):
                    dst, full = take("k", c, group)
                    product(dst, lambda k: QKV0 + k * 3 * C + 2 * C + c * P, P,
                            lambda k: act_hi[:, k, :], lambda k: act_lo[:, k, :], False).then_inc(full, 1)

            def tile_product(dst, w_at, w_n, t):
                cols = slice(t * P, (t + 1) * P)
                return product(dst, w_at, w_n, lambda k: act_hi[:, k, cols], lambda k: act_lo[:, k, cols], True)

            def qv_project(step, tiles):
                def run(group):
                    for j, t in enumerate(tiles):
                        dst, full = take(step, j, group)
                        tile_product(dst, lambda k: QKV0 + k * 3 * C, 2 * C, t).then_inc(full, 1)
                return run

            def q_turn(group):
                after(pe, "softmax_mul", group)
                turn("qT", q_tok, group)

            def e_turn(i):
                def run(group):
                    after(pe, "k_exp", group)
                    turn_back(f"eT{i}", 0, k_chan, 2 * i * P, group)
                return run

            def state_sum(i):
                def run(group):
                    read(pe, f"eT{i}", 0, group)
                    if i == 0:
                        for c in range(KC):
                            take("st3", c, group)
                    for t in range(2):
                        for c in range(KC):
                            n = 2 * i + t
                            mm = pe.matmul(att[:, FILLS["st3"][c], 0:P],
                                           q_tok[:, 2 * (i % 2) + t, c * P:(c + 1) * P],
                                           v_tok[:, n, c * P:(c + 1) * P], start=n == 0, stop=n == TPS - 1)
                            if n == TPS - 1:
                                mm.then_inc(bank_full[FILLS["st3"][c]], 1)
                    if i < 2:
                        mm.then_inc(signal["st_part"], 1)
                return run

            def attend(group):
                seq_start = shift(group, -half(group))
                for c in range(KC):
                    read(pe, "st3", c, seq_start)
                read(pe, "qT", 1, group)
                g = half(group)
                for j in range(2):
                    dst, full = take("out", j, group)
                    for t in (2 * j, 2 * j + 1):
                        for c in range(KC):
                            at = g * GT + t * P
                            mm = pe.matmul(dst[:, (t % 2) * C + c * P:(t % 2) * C + (c + 1) * P],
                                           q_chan[:, c, at:at + P], state[:, c, :], start=True, stop=True)
                    mm.then_inc(full, 1)

            def o_turn(group):
                for j in range(2):
                    read(pe, "out", j, group)
                turn("oT", n_tok, group)

            def o_project(group):
                after(pe, "oT_lo", group)
                for j in range(2):
                    dst, full = take("wo", j, group)
                    for t in (2 * j, 2 * j + 1):
                        mm = tile_product(dst[:, (t % 2) * C:(t % 2 + 1) * C], lambda k: WO0 + k * C, C, t)
                    mm.then_inc(full, 1)

            def f_turn(group):
                after(pe, "ln_f_apply", group)
                turn("fT", n_tok, group)

            def gate(group):
                for c in range(KC):
                    read(pe, "fT", c, group)
                dst, full = take("gate", 0, group)
                g = half(group)
                for t in range(TPG):
                    parts = [(part, k) for part in (f_hi, f_lo) for k in range(KC)]
                    for n, (part, k) in enumerate(parts):
                        mm = pe.matmul(dst[:, t * E:(t + 1) * E], part[:, g, k, t * P:(t + 1) * P].bitcast(F32),
                                       gate_w[:, k * E:(k + 1) * E], start=n == 0, stop=n == len(parts) - 1)
                mm.then_inc(full, 1)

            def g_turn(group):
                after(pe, "route_weight", group)
                dst, full = take("gT", 0, group)
                for t in range(TPG):
                    mm = pe.transpose(dst[0:E, t * P:(t + 1) * P], r_root[:, 3, t, :], ident)
                mm.then_inc(full, 1)

            def ffn_turn(group):
                pe.wait_ge(down_read, credited(KC, KC - 1, group))
                for j in range(2):
                    turn_back("ffn_out", j, o_chan, 2 * j * P, group)

            mine = {
                "xT": x_turn, "k": k_project, "qv01": qv_project("qv01", (0, 1)),
                "qv23": qv_project("qv23", (2, 3)), "qT": q_turn,
                "eT0": e_turn(0), "eT1": e_turn(1), "eT2": e_turn(2), "eT3": e_turn(3),
                "st0": state_sum(0), "st1": state_sum(1), "st2": state_sum(2), "st3": state_sum(3),
                "out": attend, "oT": o_turn, "wo": o_project, "fT": f_turn, "gate": gate, "gT": g_turn,
                "ffn_out": ffn_turn,
            }

            def up(j, group):
                g = half(group)
                if j == 0:
                    for c in range(KC):
                        read(pe, "fT", c, group)
                pe.wait_ge(y_rooted, credited(CH, j - 2, group))
                product(hid[:, j % 2, :], lambda k: UP0 + j * C + k * P, P,
                        lambda k: f_hi[:, g, k, :], lambda k: f_lo[:, g, k, :], False).then_inc(hid_done, 1)

            def down_product(j, group):
                if j == 0:
                    pe.wait_ge(down_read, credited(KC, -1, group))
                pe.wait_ge(y_hi_done, counted(CH, j, group))
                for n, w in enumerate((w_hi, w_lo)):
                    for c in range(KC):
                        at = DOWN0 + j * C + c * P
                        pe.matmul(down[:, c, :], w[:, at:at + P], y_hi[:, j % HB, :],
                                  start=j == 0 and n == 0, stop=False)
                pe.wait_ge(y_lo_done, credited(CH, j, group))
                for c in range(KC):
                    at = DOWN0 + j * C + c * P
                    mm = pe.matmul(down[:, c, :], w_hi[:, at:at + P], y_lo[:, j % HB, :],
                                   start=False, stop=j == CH - 1)
                mm.then_inc(y_used, 1)

            def sequence(i, even, odd):
                for g, slot in ((0, even), (1, odd)):
                    group = 2 * i + g if isinstance(i, int) else (i, g)
                    steps_at(slot, -1, i, mine)
                    for s in range(CH + LAG):
                        if s < CH:
                            up(s, group)
                        if s >= LAG:
                            down_product(s - LAG, group)
                        steps_at(slot, s, i, mine)
                    steps_at(slot, CH + LAG, i, mine)

            pe.sem_inc(y_used, CH)
            pe.wait_ge(consts_in, 48)
            pe.wait_ge(w_lo_done, UP0 // WCHUNK)
            for name, g in prologue:
                if name in mine:
                    mine[name](g)
            pe.wait_ge(w_lo_done, NWC)
            with pe.Fori(0, ITER) as i:
                sequence(i, SLOT_EVEN, SLOT_ODD)
            sequence(ITER, without_next(SLOT_EVEN), without_next(SLOT_ODD))

        @block.scalar
        def _(act):
            def ln_root(n):
                def run(group):
                    step, k = f"ln_{n}_root", LN.index(n)
                    after(act, f"ln_{n}_stats", group)
                    nc.scalar.activation(root[:, k, 0, :], root[:, k, 3, :], ACT.Ln).then_inc(signal[step], 1)
                    after(act, step, group, 1)
                    nc.scalar.activation(root[:, k, 1, :], root[:, k, 0, :], ACT.Exp, scale=-0.5).then_inc(
                        signal[step], 1)
                return run

            def x_hi(group):
                all_filled(act, 1, "xT", group)
                all_filled(act, 3, "xT", group)
                for c in range(KC):
                    src = filled(act, "xT", c, group)
                    nc.scalar.activation(act_hi[:, c, :], src, ACT.Copy).then_inc(signal["xT_hi"], 1)

            def k_out(group):
                all_filled(act, FILLS["eT3"][0], "k", group)
                g = half(group)
                for c in range(KC):
                    src = filled(act, "k", c, group)
                    nc.scalar.activation(k_chan[:, c, g * GT:(g + 1) * GT], src, ACT.Identity,
                                         bias=b_k[:, c:c + 1]).then_inc(reader_of("k", c), 1)

            def q_exponent(group):
                after(act, "softmax_sub", group)
                nc.scalar.activation(q_tok[:], q_tok[:], ACT.Exp).then_inc(signal["softmax_exp"], 1)

            def q_out(group):
                all_filled(act, FILLS["out"][1], "qT", group)
                g = half(group)
                for c in range(KC):
                    src = filled(act, "qT", c, group)
                    nc.scalar.activation(q_chan[:, c, g * GT:(g + 1) * GT], src, ACT.Copy).then_inc(
                        reader_of("qT", c), 1)

            def k_exponent(group):
                after(act, "k_max", group)
                for c in range(KC):
                    nc.scalar.activation(k_chan[:, c, :], k_chan[:, c, :], ACT.Exp, bias=kneg[:, 1, c:c + 1],
                                         accum_out=ksum[:, 0, c:c + 1]).then_inc(signal["k_exp"], 1)

            def e_out(i):
                def run(group):
                    if i >= 2:
                        after(act, "st_part", group, i - 1)
                    src = filled(act, f"eT{i}", 0, group)
                    h = 2 * (i % 2)
                    nc.scalar.activation(q_tok[:, h:h + 2, :].rearrange("p t c -> p (t c)"), src,
                                         ACT.Copy).then_inc(reader_of(f"eT{i}", 0), 1)
                return run

            def o_scale(group):
                all_filled(act, 3, "oT", group)
                all_filled(act, 1, "oT", group)
                for c in range(KC):
                    src = filled(act, "oT", c, group)
                    nc.scalar.activation(o_chan[:, c, :], src, ACT.Identity, bias=ln_b[:, c:c + 1],
                                         scale=ln_g[:, c:c + 1]).then_inc(reader_of("oT", c), 1)
                for c in range(KC):
                    read(act, "oT", c, group)
                    nc.scalar.activation(act_hi[:, c, :], o_chan[:, c, :], ACT.Copy).then_inc(signal["oT_hi"], 1)

            def f_split(group):
                wait(act, hid_done, value(lambda g: (g - 1) * CH, group))
                g = half(group)
                for c in range(KC):
                    src = filled(act, "fT", c, group)
                    nc.scalar.activation(f_hi[:, g, c, :], src, ACT.Copy).then_inc(signal["fT_hi"], 1)

            def gate_exp(group):
                src = filled(act, "gate", 0, group)
                nc.scalar.activation(r_pick[:].rearrange("p t e -> p (t e)"), src[:, 0:TPG * E], ACT.Exp,
                                     scale=-1.0).then_inc(reader_of("gate", 0), 1)

            def route_root(group):
                after(act, "route_pick", group)
                nc.scalar.activation(r_root[:, 2, :, :], r_root[:, 1, :, :], ACT.Ln).then_inc(signal["route_root"], 1)
                after(act, "route_root", group, 1)
                nc.scalar.activation(r_root[:, 2, :, :], r_root[:, 2, :, :], ACT.Exp, scale=0.5).then_inc(
                    signal["route_root"], 1)

            def g_out(group):
                wait(act, g_rows_in, value(lambda g: g * 16 * (E // EG), group))
                src = filled(act, "gT", 0, group)
                nc.scalar.activation(g_chan[:], src[0:E, :], ACT.Copy).then_inc(reader_of("gT", 0), 1)

            def ffn_evac(group):
                act.wait_ge(y_used, credited(CH, CH - 1, group))
                runs_ahead = value(lambda g: sum(s == "oT" for s, _ in order[:place["ffn_evac", g]]), group)
                act.wait_ge(signal["oT_lo"], runs_ahead * SIGNALS["oT_lo"])
                for c in range(KC):
                    nc.scalar.activation(o_chan[:, c, :], down[:, c, :], ACT.Copy).then_inc(down_read, 1)

            mine = {
                **{f"ln_{n}_root": ln_root(n) for n in LN}, "xT": x_hi, "k": k_out, "softmax_exp": q_exponent,
                "qT": q_out, "k_exp": k_exponent, "eT0": e_out(0), "eT1": e_out(1), "eT2": e_out(2),
                "eT3": e_out(3), "oT": o_scale, "fT": f_split, "gate": gate_exp, "route_root": route_root,
                "gT": g_out, "ffn_evac": ffn_evac,
            }

            def square(j, group):
                act.wait_ge(y_rooted, credited(CH, j, group))
                nc.scalar.activation(y[:, j % YB, :], y[:, j % YB, :], ACT.Square).then_inc(y_squared, 1)
                act.wait_ge(y_squared, counted(CH, j, group))
                act.wait_ge(y_used, credited(CH, j - HB, group))
                nc.scalar.activation(y_hi[:, j % HB, :], y[:, j % YB, :], ACT.Copy).then_inc(y_hi_done, 1)

            def sequence(i, even, odd):
                for g, slot in ((0, even), (1, odd)):
                    group = 2 * i + g if isinstance(i, int) else (i, g)
                    steps_at(slot, -1, i, mine)
                    for s in range(CH + LAG):
                        if s < CH:
                            square(s, group)
                        steps_at(slot, s, i, mine)
                    steps_at(slot, CH + LAG, i, mine)

            def split_weights(c):
                act.wait_ge(w_in[c % STAGE], 16 * (c // STAGE + 1))
                nc.scalar.activation(w_hi[:, c * WCHUNK:(c + 1) * WCHUNK], stage[:, c % STAGE, :],
                                     ACT.Copy).then_inc(w_hi_done, 1)

            mine["split"] = split_weights

            nc.scalar.preload_act_table_set("natural_log_exp_and_others")
            act.sem_inc(down_read, KC)
            for c in range(UP0 // WCHUNK):
                split_weights(c)
            act.wait_ge(consts_in, 48)
            for name, g in prologue:
                if name in mine:
                    mine[name](g)
            with act.Fori(0, ITER) as i:
                sequence(i, SLOT_EVEN, SLOT_ODD)
            sequence(ITER, without_next(SLOT_EVEN), without_next(SLOT_ODD))

        @block.vector
        def _(dve):
            v = nc.vector

            class Run:

                def __init__(self, step, group):
                    self.step, self.group, self.n = step, group, 0

                def did(self, instruction):
                    instruction.then_inc(signal[self.step], 1)
                    self.n += 1

                def settle(self):
                    after(dve, self.step, self.group, self.n)

                def then(self, instruction):
                    self.did(instruction)
                    self.settle()

                def end(self):
                    assert self.n == SIGNALS[self.step], (self.step, self.n)

            def ln_stats(n):
                def run(group):
                    k, r, g = LN.index(n), Run(f"ln_{n}_stats", group), half(group)
                    if n == "x":
                        dve.wait_ge(x_in, value(lambda q: 16 * (q + 1), group))
                    for t in range(TPG):
                        if n == "x":
                            src = x_tok[:, t, :]
                        elif n == "o":
                            if t % 2 == 0:
                                bank = filled(dve, "out", t // 2, group)
                            src = bank[:, (t % 2) * C:(t % 2 + 1) * C]
                        else:
                            if t == 0:
                                for j in range(2):
                                    read(dve, "wo", j, group)
                            src = x1[:, g * TPG + t, :]
                        last = v.bn_stats(stats[:, k, t, :], src)
                    r.then(last)
                    stand_alone(dve)
                    for t in range(TPG):
                        last = v.bn_aggr(mv[:, k, t, :], stats[:, k, t, :])
                    r.then(last)
                    r.did(v.tensor_scalar(root[:, k, 3, :], mv[:, k, :, 1], EPS, None, ALU.add))
                    r.end()
                return run

            def ln_apply(n):
                def run(group):
                    k, r, g = LN.index(n), Run(f"ln_{n}_apply", group), half(group)
                    after(dve, f"ln_{n}_root", group)
                    r.then(v.tensor_tensor(root[:, k, 2, :], root[:, k, 1, :], root[:, k, 1, :], ALU.mult))
                    r.then(v.scalar_tensor_tensor(out=root[:, k, 2, :], in0=root[:, k, 2, :], scalar=-0.5,
                                                  in1=root[:, k, 3, :], op0=ALU.mult, op1=ALU.mult))
                    r.then(v.scalar_tensor_tensor(out=root[:, k, 2, :], in0=root[:, k, 2, :], scalar=1.5,
                                                  in1=root[:, k, 1, :], op0=ALU.add, op1=ALU.mult))
                    for t in range(TPG):
                        if n == "o":
                            bank = att[:, FILLS["out"][t // 2], :]
                            src, dst = bank[:, (t % 2) * C:(t % 2 + 1) * C], n_tok[:, t, :]
                        elif n == "x":
                            src = dst = x_tok[:, t, :]
                        else:
                            src, dst = x1[:, g * TPG + t, :], n_tok[:, t, :]
                        last = v.tensor_scalar(dst, src, mv[:, k, t, 0:1], root[:, k, 2, t:t + 1],
                                               ALU.subtract, ALU.mult)
                        if n == "o" and t % 2:
                            last.then_inc(reader_of("out", t // 2), 1)
                    if n != "o":
                        r.did(last)
                    r.end()
                return run

            def x_lo(group):
                for c in range(KC):
                    after(dve, "xT_hi", group, c + 1)
                    v.tensor_tensor(act_lo[:, c, :], att[:, FILLS["xT"][c], :], act_hi[:, c, :].bitcast(F32),
                                    ALU.subtract).then_inc(reader_of("xT", c), 1)

            def k_top(group):
                r = Run("k_top", group)
                g = half(group)
                for c in range(KC):
                    read(dve, "k", c, group)
                    r.did(v.tensor_reduce(kmax[:, c, g:g + 1], k_chan[:, c, g * GT:(g + 1) * GT], AX.X, ALU.max))
                r.end()

            def qv_out(step, tiles):
                def run(group):
                    all_filled(dve, FILLS["qT"][1], step, group)
                    all_filled(dve, FILLS["st3"][1], step, group)
                    for j, t in enumerate(tiles):
                        src = filled(dve, step, j, group)
                        v.tensor_tensor(q_tok[:, t, :], src[:, 0:C], b_qv[:, 0:C], ALU.add)
                        v.tensor_tensor(v_tok[:, half(group) * TPG + t, :], src[:, C:2 * C], b_qv[:, C:2 * C],
                                        ALU.add).then_inc(reader_of(step, j), 1)
                return run

            def softmax_max(group):
                r = Run("softmax_max", group)
                for step in ("qv01", "qv23"):
                    for j in range(2):
                        read(dve, step, j, group)
                r.did(v.tensor_reduce(qmax[:], q_tok[:].rearrange("p t (h d) -> p (t h) d", d=HD), AX.X, ALU.max))
                r.end()

            def softmax_sum(group):
                r = Run("softmax_sum", group)
                after(dve, "softmax_exp", group)
                r.then(v.tensor_reduce(qsum[:, 0, :], q_tok[:].rearrange("p t (h d) -> p (t h) d", d=HD),
                                       AX.X, ALU.add))
                r.did(v.reciprocal(qsum[:, 1, :], qsum[:, 0, :]))
                r.end()

            def k_max(group):
                r = Run("k_max", group)
                after(dve, "k_top", shift(group, 1))
                r.then(v.tensor_tensor(kneg[:, 0, :], kmax[:, :, 0], kmax[:, :, 1], ALU.max))
                r.did(v.tensor_scalar(kneg[:, 1, :], kneg[:, 0, :], -1.0, None, ALU.mult))
                r.end()

            def k_sum(group):
                r = Run("k_sum", group)
                after(dve, "k_exp", group)
                r.did(v.reciprocal(ksum[:, 1, :], ksum[:, 0, :]))
                r.end()

            def state_out(group):
                all_filled(dve, FILLS["out"][1], "state", group)
                after(dve, "k_sum", group)
                for c in range(KC):
                    src = filled(dve, "st3", c, group)
                    v.scalar_tensor_tensor(out=state[:, c, :], in0=src[:, 0:P], scalar=ksum[:, 1, c:c + 1],
                                           in1=same_head, op0=ALU.mult, op1=ALU.mult).then_inc(
                        reader_of("st3", c), 1)

            def o_lo(group):
                r = Run("oT_lo", group)
                for c in range(KC):
                    after(dve, "oT_hi", group, c + 1)
                    r.did(v.tensor_tensor(act_lo[:, c, :], o_chan[:, c, :], act_hi[:, c, :].bitcast(F32),
                                          ALU.subtract))
                r.end()

            def residual_add(group):
                after(dve, "residual", group)
                for j in range(2):
                    src = filled(dve, "wo", j, group)
                    at = half(group) * TPG + 2 * j
                    part = x1[:, at:at + 2, :].rearrange("p t c -> p (t c)")
                    v.tensor_tensor(part, src, part, ALU.add).then_inc(reader_of("wo", j), 1)

            def f_lo_out(group):
                for c in range(KC):
                    after(dve, "fT_hi", group, c + 1)
                    v.tensor_tensor(f_lo[:, half(group), c, :], att[:, FILLS["fT"][c], :],
                                    f_hi[:, half(group), c, :].bitcast(F32), ALU.subtract).then_inc(
                        reader_of("fT", c), 1)

            def route_pick(group):
                r = Run("route_pick", group)
                read(dve, "gate", 0, group)
                scores = r_list[:, :, 0:E]
                by_group = scores.rearrange("p t (g e) -> p t g e", e=EG)
                pairs = r_half[:].rearrange("p h (t g) e -> p h t g e", g=EG)
                r.then(v.tensor_scalar(r_pick[:], r_pick[:], 1.0, None, ALU.add))
                r.then(v.reciprocal(r_score[:], r_pick[:]))
                r.then(v.tensor_tensor(scores, r_score[:], b_e.unsqueeze(1).broadcast_to([P, TPG, E]), ALU.add))
                r.did(v.tensor_tensor(pairs[:, 0], by_group[:, :, :, 0::2], by_group[:, :, :, 1::2], ALU.max))
                r.then(v.tensor_tensor(pairs[:, 1], by_group[:, :, :, 0::2], by_group[:, :, :, 1::2], ALU.min))
                r.did(v.tensor_tensor(r_pair[:, :, 0:2], r_half[:, 0], r_half[:, 1], ALU.add))
                r.then(v.tensor_tensor(r_pair[:, :, 2], r_half[:, 0, :, 0], r_half[:, 0, :, 1], ALU.add))
                best = r_group[:, 0]
                r.then(v.tensor_reduce(best.rearrange("p t g -> p (t g)"), r_pair[:], AX.X, ALU.max))
                other = best.unsqueeze(2).broadcast_to([P, TPG, EG, EG])
                own = best.unsqueeze(3).broadcast_to([P, TPG, EG, EG])
                above = r_above[:].rearrange("p n (t g) o -> p n t g o", g=EG)
                r.did(v.tensor_tensor(above[:, 0], other, own, ALU.is_gt))
                r.then(v.tensor_tensor(above[:, 1], other, own, ALU.is_equal))
                flat_above = r_above[:].rearrange("p n (t g) o -> p n t (g o)", g=EG)
                r.then(v.tensor_tensor(flat_above[:, 1], flat_above[:, 1],
                                       earlier.unsqueeze(1).broadcast_to([P, TPG, EG * EG]), ALU.mult))
                r.then(v.tensor_tensor(r_above[:, 0], r_above[:, 0], r_above[:, 1], ALU.add))
                keep = r_group[:, 1]
                r.then(v.tensor_reduce(keep.rearrange("p t g -> p (t g)"), r_above[:, 0], AX.X, ALU.add))
                r.then(v.tensor_scalar(keep, keep, 1.5, None, ALU.is_lt))
                r.then(v.tensor_tensor(by_group, by_group, keep.unsqueeze(3).broadcast_to([P, TPG, EG, EG]),
                                       ALU.mult))
                stand_alone(dve)
                for t in range(TPG):
                    last = v.max(r_best[:, t, :], r_list[:, t, 0:E])
                r.then(last)
                r.then(v.memset(r_best[:, :, 4:8], NONE))
                stand_alone(dve)
                for t in range(TPG):
                    last = v.match_replace(r_left[:, t, :], r_best[:, t, :], r_list[:, t, :], -NONE)
                r.then(last)
                r.then(v.tensor_scalar(r_pick[:], r_left[:, :, 0:E], -NONE, None, ALU.is_equal))
                r.then(v.tensor_tensor(r_root[:, 0], r_score[:], r_pick[:], ALU.mult))
                r.then(v.tensor_reduce(r_sum[:, 0, :], r_root[:, 0], AX.X, ALU.add))
                r.then(v.tensor_scalar(r_sum[:, 0, :], r_sum[:, 0, :], 1e-20, None, ALU.add))
                r.then(v.reciprocal(r_sum[:, 1, :], r_sum[:, 0, :]))
                r.then(v.scalar_tensor_tensor(out=r_root[:, 0], in0=r_root[:, 0], scalar=2.5,
                                              in1=r_sum[:, 1, :].unsqueeze(2).broadcast_to([P, TPG, E]),
                                              op0=ALU.mult, op1=ALU.mult))
                r.did(v.tensor_scalar(r_root[:, 1], r_root[:, 0], 1e-18, None, ALU.max))
                r.end()

            def route_weight(group):
                r = Run("route_weight", group)
                after(dve, "route_root", group)
                r.then(v.reciprocal(r_root[:, 1], r_root[:, 2]))
                r.then(v.tensor_tensor(r_root[:, 1], r_root[:, 0], r_root[:, 1], ALU.mult))
                r.then(v.tensor_tensor(r_root[:, 1], r_root[:, 1], r_root[:, 2], ALU.add))
                r.did(v.scalar_tensor_tensor(out=r_root[:, 3], in0=r_root[:, 1], scalar=0.5, in1=r_pick[:],
                                             op0=ALU.mult, op1=ALU.mult))
                r.end()

            def ffn_add(group):
                for j in range(2):
                    src = filled(dve, "ffn_out", j, group)
                    at = half(group) * TPG + 2 * j
                    part = x1[:, at:at + 2, :].rearrange("p t c -> p (t c)")
                    v.tensor_tensor(part, src, part, ALU.add).then_inc(reader_of("ffn_out", j), 1)

            mine = {
                **{f"ln_{n}_stats": ln_stats(n) for n in LN}, **{f"ln_{n}_apply": ln_apply(n) for n in LN},
                "xT": x_lo, "k": k_top, "qv01": qv_out("qv01", (0, 1)), "qv23": qv_out("qv23", (2, 3)),
                "softmax_max": softmax_max, "softmax_sum": softmax_sum, "k_max": k_max, "k_sum": k_sum,
                "state": state_out, "oT": o_lo, "wo": residual_add, "fT": f_lo_out,
                "route_pick": route_pick, "route_weight": route_weight, "ffn_out": ffn_add,
            }

            def weigh(j, group):
                dve.wait_ge(hid_done, counted(CH, j, group))
                dve.wait_ge(y_lo_done, credited(CH, j - YB, group))
                if j < E:
                    dve.wait_ge(g_all_done, counted(E, j, group))
                    v.scalar_tensor_tensor(out=y[:, j % YB, :], in0=hid[:, j % 2, :], scalar=0.0,
                                           in1=g_all[:, j % GB, :], op0=ALU.max, op1=ALU.mult).then_inc(y_rooted, 1)
                else:
                    v.tensor_scalar(y[:, j % YB, :], hid[:, j % 2, :], 0.0, None, ALU.max).then_inc(y_rooted, 1)

            def split(j, group):
                dve.wait_ge(y_hi_done, counted(CH, j, group))
                v.tensor_tensor(y_lo[:, j % HB, :], y[:, j % YB, :], y_hi[:, j % HB, :].bitcast(F32),
                                ALU.subtract).then_inc(y_lo_done, 1)

            def sequence(i, even, odd):
                for g, slot in ((0, even), (1, odd)):
                    group = 2 * i + g if isinstance(i, int) else (i, g)
                    steps_at(slot, -1, i, mine)
                    for s in range(CH + LAG):
                        if s < CH:
                            weigh(s, group)
                        if 1 <= s <= CH:
                            split(s - 1, group)
                        steps_at(slot, s, i, mine)
                    steps_at(slot, CH + LAG, i, mine)

            def split_weights(c):
                dve.wait_ge(w_hi_done, c + 1)
                at = slice(c * WCHUNK, (c + 1) * WCHUNK)
                v.tensor_tensor(w_lo[:, at], stage[:, c % STAGE, :], w_hi[:, at].bitcast(F32),
                                ALU.subtract).then_inc(w_lo_done, 1)

            mine["split"] = split_weights

            dve.sem_inc(y_rooted, CH)
            dve.sem_inc(y_lo_done, CH)
            v.memset(r_list[:, :, E:E + 4], NONE).then_inc(list_end, 1)
            for c in range(UP0 // WCHUNK):
                split_weights(c)
            dve.wait_ge(consts_in, 48)
            dve.wait_ge(list_end, 1)
            for name, g in prologue:
                if name in mine:
                    mine[name](g)
            with dve.Fori(0, ITER) as i:
                sequence(i, SLOT_EVEN, SLOT_ODD)
            sequence(ITER, without_next(SLOT_EVEN), without_next(SLOT_ODD))

        @block.gpsimd
        def _(pool):
            def softmax_sub(group):
                after(pool, "softmax_max", group)
                heads = q_tok[:].rearrange("p t (h d) -> p (t h) d", d=HD)
                nc.gpsimd.tensor_tensor(heads, heads, qmax[:].unsqueeze(2).broadcast_to([P, TPG * HEADS, HD]),
                                        ALU.subtract).then_inc(signal["softmax_sub"], 1)
                after(pool, "softmax_sub", group)

            def softmax_mul(group):
                after(pool, "softmax_sum", group)
                heads = q_tok[:].rearrange("p t (h d) -> p (t h) d", d=HD)
                nc.gpsimd.tensor_tensor(heads, heads, qsum[:, 1, :].unsqueeze(2).broadcast_to([P, TPG * HEADS, HD]),
                                        ALU.mult).then_inc(signal["softmax_mul"], 1)
                after(pool, "softmax_mul", group)

            def residual(group):
                pool.wait_ge(res_in[half(group)], value(lambda g: 16 * (g // 2 + 1), group))
                at = half(group) * TPG
                part = x1[:, at:at + TPG, :]
                nc.gpsimd.tensor_tensor(part, part, b_o.unsqueeze(1).broadcast_to([P, TPG, C]),
                                        ALU.add).then_inc(signal["residual"], 1)
                after(pool, "residual", group)

            mine = {"softmax_sub": softmax_sub, "softmax_mul": softmax_mul, "residual": residual}

            def broadcast(e, group):
                if e == 0:
                    pool.wait_ge(g_rows_in, value(lambda g: 16 * (E // EG) * (g + 1), group))
                pool.wait_ge(y_rooted, credited(CH, e - GB if e >= GB else E + e - GB - CH, group))
                stand_alone(pool)
                row = 32 * (e // EG)
                nc.gpsimd.partition_broadcast(g_all[:, e % GB, :], g_rows[row:row + 1, e % EG, :], P).then_inc(
                    g_all_done, 1)
                pool.wait_ge(g_all_done, counted(E, e, group))
                stand_alone(pool)

            def sequence(i, even, odd):
                for g, slot in ((0, even), (1, odd)):
                    group = 2 * i + g if isinstance(i, int) else (i, g)
                    steps_at(slot, -1, i, mine)
                    for s in range(CH + LAG):
                        if s < E:
                            broadcast(s, group)
                        steps_at(slot, s, i, mine)
                    steps_at(slot, CH + LAG, i, mine)

            pool.wait_ge(consts_in, 48)
            for name, g in prologue:
                if name in mine:
                    mine[name](g)
            with pool.Fori(0, ITER) as i:
                sequence(i, SLOT_EVEN, SLOT_ODD)
            sequence(ITER, without_next(SLOT_EVEN), without_next(SLOT_ODD))


def kernel(L0_attn_x, L0_attn_Wq, L0_attn_bq, L0_attn_Wk, L0_attn_bk, L0_attn_Wv, L0_attn_bv, L0_attn_Wo,
           L0_attn_bo, L0_attn_ln_g, L0_attn_ln_b, L0_ffn_gate_w, L0_ffn_bias_e, L0_ffn_up_w, L0_ffn_down_w,
           L0_ffn_shared_up, L0_ffn_shared_down):
    import numpy as np
    import concourse.bacc as bacc
    from concourse.bass_utils import run_bass_kernel_spmd

    B, N, C = L0_attn_x.shape
    halves = C // P

    def by_channel(w):
        return np.asarray(w).T.reshape(halves, P, -1).transpose(1, 0, 2)

    qvk = np.concatenate([by_channel(L0_attn_Wq), by_channel(L0_attn_Wv), by_channel(L0_attn_Wk)], axis=2)
    ups = np.concatenate([np.asarray(L0_ffn_up_w).reshape(-1, C), np.asarray(L0_ffn_shared_up)], axis=0)
    chunks = ups.shape[0] // P
    ups = ups.reshape(chunks, P, halves, P).transpose(3, 0, 2, 1)
    downs = np.concatenate([np.asarray(L0_ffn_down_w),
                            np.asarray(L0_ffn_shared_down).reshape(C, -1, P).transpose(1, 0, 2)], axis=0)
    downs = downs.transpose(2, 0, 1)
    weights = np.concatenate([a.reshape(P, -1) for a in (qvk, by_channel(L0_attn_Wo), ups, downs)], axis=1)
    rows = np.concatenate([np.asarray(a) for a in (L0_attn_bq, L0_attn_bv, L0_attn_bo, L0_ffn_bias_e)])
    columns = np.concatenate([np.asarray(a).reshape(halves, P).T for a in (L0_attn_bk, L0_attn_ln_g, L0_attn_ln_b)]
                             + [by_channel(L0_ffn_gate_w).reshape(P, -1)], axis=1)
    head = np.arange(P) // 16
    earlier = (np.arange(4)[None, :] < np.arange(4)[:, None]).reshape(1, -1).repeat(P, axis=0)
    masks = np.concatenate([np.eye(P), head[:, None] == head[None, :], earlier], axis=1).astype(np.float32)

    arrays = {"x": np.asarray(L0_attn_x).reshape(B * N, C), "weights": weights, "rows": rows,
              "columns": columns, "masks": masks}
    arrays = {k: np.ascontiguousarray(a) for k, a in arrays.items()}
    nc = bacc.Bacc("TRN2", target_bir_lowering=False, num_devices=1)
    ins = [nc.dram_tensor(k, a.shape, F32, kind="ExternalInput").ap() for k, a in arrays.items()]
    out = nc.dram_tensor("out", (B * N, C), F32, kind="ExternalOutput").ap()
    layer_kernel(nc, *ins, out)
    result = run_bass_kernel_spmd(nc, [arrays], core_ids=[0])
    return result.results[0]["out"].reshape(B, N, C)
```

```python
from contextlib import ExitStack

import concourse.bass as bass
from concourse import mybir

F32 = mybir.dt.float32
F32R = mybir.dt.float32r
ALU = mybir.AluOpType
ACT = mybir.ActivationFunctionType
AX = mybir.AxisListType

P = 128
EPS = 1e-5
TPG = 4
GT = TPG * P
BANK = 512
LAG = 2
WCHUNK = 512
STAGE = 4

FILLS = {
    "xT": (0, 1), "k": (3, 2), "q": (0, 1), "v": (2, 3), "qT": (0, 1), "eT0": (0,), "eT1": (1,),
    "eT2": (0,), "eT3": (1,), "st3": (3, 2), "out": (0, 1), "oT": (0, 2), "wo": (2, 3), "fT": (2, 3),
    "gate": (2,), "gT": (3,),
}
SIGNALS = {
    "ln_x_stats": 3, "ln_o_stats": 3, "ln_f_stats": 3,
    "ln_x_root": 2, "ln_o_root": 2, "ln_f_root": 2,
    "ln_x_apply": 4, "ln_o_apply": 4, "ln_f_apply": 4,
    "ln_x_norm": 1, "ln_f_norm": 1,
    "xT_hi": 2, "oT_hi": 2, "fT_hi": 2,
    "oT_lo": 2, "k_top": 2, "softmax_max": 1,
    "softmax_sub": 1, "softmax_mul": 1, "residual": 1,
    "softmax_exp": 1, "k_exp": 2,
    "softmax_sum": 2, "k_max": 2, "k_sum": 1,
    "st_part": 2,
    "route_group": 15, "route_pick": 10, "route_weight": 4,
    "logits": 1,
    "gate_exp": 1, "route_root": 2,
}
PROJECTIONS = ("k", "q", "v", "wo")
ONCE_A_SEQUENCE = {"k_exp", "k_max", "k_sum", "st_part"}

PROLOGUE = [
    ("ln_x_stats", 0), ("split", 0), ("split", 1), ("ln_x_root", 0), ("ln_x_stats", 1), ("ln_x_root", 1),
    ("ln_x_apply", 0), ("split", 2), ("xT", 0), ("ln_x_apply", 1), ("consts", 0), ("split", 3),
    ("w_ready", 3), ("split", 4), ("k", 0), ("v", 0), ("q", 0), ("xT", 1), ("k", 1), ("split", 5),
    ("w_ready", 4), ("softmax_max", 0), ("softmax_sub", 0), ("split", 6), ("split", 7), ("softmax_exp", 0),
    ("softmax_sum", 0), ("softmax_mul", 0), ("k_max", 0), ("k_exp", 0), ("split", 8), ("v", 1),
    ("split", 9), ("k_sum", 0), ("qT", 0), ("split", 10), ("eT0", 0), ("eT1", 0), ("st0", 0), ("split", 11),
    ("st1", 0), ("split", 12), ("eT2", 0), ("eT3", 0), ("residual", 0), ("st2", 0), ("st3", 0),
    ("state", 0), ("split", 13), ("q", 1), ("out", 0), ("split", 14), ("ln_o_stats", 0), ("ln_o_root", 0),
    ("ln_o_apply", 0), ("softmax_max", 1), ("softmax_sub", 1), ("split", 15), ("oT", 0), ("softmax_exp", 1),
    ("split", 16), ("softmax_sum", 1), ("split", 17), ("wo", 0), ("split", 18), ("ln_f_stats", 0),
    ("ln_f_root", 0), ("ln_f_apply", 0), ("split", 19), ("fT", 0), ("softmax_mul", 1), ("gate", 0),
    ("route_group", 0), ("route_pick", 0), ("split", 20), ("split", 21), ("qT", 1), ("split", 22),
    ("split", 23), ("route_root", 0), ("route_weight", 0),
]
SLOTS = {
    0: [("out", 1), ("load_x", 2), ("ln_o_stats", 1), ("gT", 0), ("ln_o_root", 1)],
    1: [("ln_o_apply", 1)],
    2: [("ln_x_stats", 2)],
    3: [("ln_x_root", 2)],
    4: [("residual", 1), ("oT", 1)],
    5: [("ln_x_apply", 2)],
    6: [("wo", 1), ("ln_f_stats", 1), ("xT", 2)],
    7: [("ln_f_root", 1), ("load_x", 3)],
    8: [("k", 2), ("ln_f_apply", 1)],
    9: [("ln_x_stats", 3), ("q", 2), ("fT", 1), ("softmax_max", 2)],
    10: [("gate", 1), ("softmax_sub", 2), ("route_group", 1)],
    11: [("ln_x_root", 3), ("v", 2)],
    12: [("softmax_exp", 2), ("route_pick", 1), ("route_root", 1)],
    13: [("route_weight", 1)],
    15: [("ln_x_apply", 3), ("softmax_sum", 2)],
    17: [("gT", 1), ("xT", 3), ("softmax_mul", 2)],
    18: [("k", 3), ("qT", 2)],
    19: [("q", 3), ("k_max", 2)],
    20: [("k_exp", 2)],
    21: [("ffn_out", 0)],
    23: [("softmax_max", 3), ("v", 3), ("eT0", 2)],
    24: [("st0", 2)],
    25: [("eT1", 2), ("softmax_sub", 3)],
    26: [("eT2", 2), ("st1", 2), ("softmax_exp", 3), ("eT3", 2), ("st2", 2)],
    27: [("k_sum", 2), ("st3", 2), ("softmax_sum", 3), ("state", 2)],
    28: [("out", 2), ("ln_o_stats", 2)],
    29: [("softmax_mul", 3), ("ln_o_root", 2)],
    30: [("residual", 2), ("ln_o_apply", 2)],
    31: [("oT", 2)],
    33: [("wo", 2), ("ln_f_stats", 2), ("ln_f_root", 2)],
    34: [("ln_f_apply", 2)],
    36: [("fT", 2)],
    37: [("gate", 2), ("qT", 3), ("route_group", 2)],
    39: [("route_pick", 2)],
    40: [("route_root", 2)],
    41: [("route_weight", 2), ("ffn_out", 1)],
}


def without_next(slot):
    return {s: [x for x in steps if x[1] < 2] for s, steps in slot.items()}


def layer_kernel(nc, x, weights, rows, columns, masks, out):
    TOKENS, C = x.shape
    E, EG = 16, 4
    CH = weights.shape[1] // (2 * C) - 4
    SH = CH - E
    KC = C // P
    HD = 16
    HEADS = C // HD
    GROUPS = TOKENS // GT
    SEQS = GROUPS // 2
    TPS = 2 * TPG
    ITER = SEQS - 1
    NW = weights.shape[1]
    NWC = NW // WCHUNK
    QKV0, WO0, UP0 = 0, KC * 3 * C, KC * 4 * C
    DOWN0 = UP0 + CH * C
    NONE = -3.0e38

    def flat(i, slots):
        return [(n, g + 2 * i) for s in sorted(slots) for n, g in slots[s]]

    order = list(PROLOGUE)
    for i in range(ITER):
        order += flat(i, SLOTS)
    order += flat(ITER, without_next(SLOTS))
    place = {x: n for n, x in enumerate(order)}

    def value(f, group):
        if isinstance(group, tuple):
            i, g = group
            step = f(g + 2) - f(g)
            return i * step + f(g) if step else f(g)
        return f(group)

    def shift(group, by):
        return (group[0], group[1] + by) if isinstance(group, tuple) else group + by

    def half(group):
        return (group[1] if isinstance(group, tuple) else group) % 2

    def ahead(step, group, bank):
        return value(lambda g: sum(FILLS.get(s, ()).count(bank) for s, _ in order[:place[step, g]]), group)

    def fill(step, j, group):
        bank = FILLS[step][j]
        return bank, ahead(step, group, bank) + FILLS[step][:j + 1].count(bank)

    def wait(eng, sem, v):
        if not isinstance(v, int) or v > 0:
            eng.wait_ge(sem, v)

    with ExitStack() as ctx:
        def sb(name, shape, dt=F32):
            return ctx.enter_context(nc.sbuf_tensor(name, shape, dt))

        def sem(name):
            return ctx.enter_context(nc.semaphore(name))

        w_hi = sb("w_hi", [P, NW], F32R)
        w_lo = sb("w_lo", [P, NW], F32R)
        x_tok = sb("x_tok", [P, TPG, C])
        q_tok = sb("q_tok", [P, TPG, C])
        v_tok = sb("v_tok", [P, TPS, C])
        n_tok = sb("n_tok", [P, TPG, C])
        act_hi = sb("act_hi", [P, KC, GT], F32R)
        act_lo = sb("act_lo", [P, KC, GT], F32R)
        k_chan = sb("k_chan", [P, KC, 2 * GT])
        q_chan = sb("q_chan", [P, KC, 2 * GT])
        o_chan = sb("o_chan", [P, KC, GT])
        x1 = sb("x1", [P, TPS, C])
        f_hi = sb("f_hi", [P, 2, KC, GT], F32R)
        f_lo = sb("f_lo", [P, 2, KC, GT], F32R)
        g_chan = sb("g_chan", [E, GT])
        g_rows = sb("g_rows", [P, EG, GT])
        GB, YB, HB = 2, 3, 2
        g_all = sb("g_all", [P, GB, GT])
        y = sb("y", [P, YB, GT])
        y_hi = sb("y_hi", [P, HB, GT], F32R)
        y_lo = sb("y_lo", [P, HB, GT], F32R)
        gate_parts = sb("gate_parts", [P, KC, 2, E], F32R)
        state = sb("state", [P, KC, P])
        row_c = sb("row_c", [P, rows.shape[0]])
        col_c = sb("col_c", [P, columns.shape[1]])
        mask_c = sb("mask_c", [P, masks.shape[1]])
        LN = ("x", "o", "f")
        stats = sb("stats", [P, 3, TPG, 6])
        mv = sb("mv", [P, 3, TPG, 2])
        root = sb("root", [P, 3, 4, TPG])
        qmax = sb("qmax", [P, TPG * HEADS])
        qsum = sb("qsum", [P, 2, TPG * HEADS])
        kmax = sb("kmax", [P, KC, 2])
        kneg = sb("kneg", [P, 2, KC])
        ksum = sb("ksum", [P, 2, KC])
        r_score = sb("r_score", [P, TPG, E])
        r_pick = sb("r_pick", [P, TPG, E])
        r_half = sb("r_half", [P, 2, TPG * EG, 2])
        r_pair = sb("r_pair", [P, TPG * EG, 3])
        r_group = sb("r_group", [P, 2, TPG, EG])
        r_above = sb("r_above", [P, 2, TPG * EG, EG])
        r_list = sb("r_list", [P, TPG, E + 4])
        r_best = sb("r_best", [P, TPG, 8])
        r_left = sb("r_left", [P, TPG, E + 4])
        r_sum = sb("r_sum", [P, 2, TPG])
        r_root = sb("r_root", [P, 4, TPG, E])

        b_qv, b_o, b_e = row_c[:, 0:2 * C], row_c[:, 2 * C:3 * C], row_c[:, 3 * C:3 * C + E]
        b_k, ln_g, ln_b = col_c[:, 0:KC], col_c[:, KC:2 * KC], col_c[:, 2 * KC:3 * KC]
        gate_w = col_c[:, 3 * KC:3 * KC + KC * E]
        ident, same_head, earlier = mask_c[:, 0:P], mask_c[:, P:2 * P], mask_c[:, 2 * P:2 * P + EG * EG]
        stage = g_rows

        hid = ctx.enter_context(nc.psum_tensor("hid", [P, 2, BANK], F32))
        down = ctx.enter_context(nc.psum_tensor("down", [P, KC, BANK], F32))
        att = ctx.enter_context(nc.psum_tensor("att", [P, 4, BANK], F32))

        mask_in = sem("mask_in")
        consts_in = sem("consts_in")
        w_in = [sem(f"w_in{k}") for k in range(STAGE)]
        w_hi_done = sem("w_hi_done")
        w_lo_done = sem("w_lo_done")
        x_in = sem("x_in")
        res_in = [sem(f"res_in{k}") for k in range(2)]
        stored = [sem(f"stored{k}") for k in range(2)]
        bank_full = [sem(f"bank_full{k}") for k in range(4)]
        bank_read = [sem(f"bank_read{k}") for k in range(4)]
        signal = {s: sem(s) for s in SIGNALS}
        g_rows_in = sem("g_rows_in")
        g_all_done = sem("g_all_done")
        gate_parts_done = sem("gate_parts_done")
        list_end = sem("list_end")
        hid_done = sem("hid_done")
        y_rooted = sem("y_rooted")
        y_squared = sem("y_squared")
        y_hi_done = sem("y_hi_done")
        y_lo_done = sem("y_lo_done")
        y_used = sem("y_used")
        down_read = sem("down_read")

        passed = {e: sem(f"passed_{e.name}") for e in (nc.sync.engine, nc.vector.engine, nc.gpsimd.engine)}

        def runs(step, group):
            per = SIGNALS[step]
            return value(lambda g: (g // 2 if step in ONCE_A_SEQUENCE else g) * per, group)

        def after(eng, step, group, k=None):
            eng.wait_ge(signal[step], runs(step, group) + (SIGNALS[step] if k is None else k))

        def filled(eng, step, j, group):
            bank, n = fill(step, j, group)
            eng.wait_ge(bank_full[bank], n)
            return att[:, bank, :]

        def read(eng, step, j, group):
            bank, n = fill(step, j, group)
            eng.wait_ge(bank_read[bank], n)

        def all_used(eng, users, step, group):
            for bank in sorted({FILLS[user][-1] for user in users}):
                wait(eng, bank_full[bank], ahead(step, group, bank))

        def reader_of(step, j):
            return bank_read[FILLS[step][j]]

        def credited(per_group, k, group):
            return value(lambda g: (g + 1) * per_group + k + 1, group)

        def counted(per_group, k, group):
            return value(lambda g: g * per_group + k + 1, group)

        def chunk(s, i):
            return s % CH, 2 * i + s // CH if isinstance(i, int) else (i, s // CH)

        def steps_at(slots, s, i, mine):
            for name, g in slots.get(s, ()):
                if name in mine:
                    mine[name](2 * i + g if isinstance(i, int) else (i, g))

        def stand_alone(eng):
            eng.sem_inc(passed[eng.engine], 1)

        def raw_x(group):
            if isinstance(group, int) and group < 2:
                return x1[:, half(group) * TPG:(half(group) + 1) * TPG, :]
            return x_tok[:]

        def norm_place(n, group):
            return LN.index("o") if (n, group) == ("x", 1) else LN.index(n)

        def x_turned(group):
            return (f_hi[:, 1], f_lo[:, 1]) if group == 1 else (act_hi[:], act_lo[:])

        def tokens(dram, group):
            return dram[bass.ds(value(lambda g: g * GT, group), GT), :].rearrange("(t p) c -> p t c", p=P)

        block = ctx.enter_context(nc.Block())

        @block.sync
        def _(sp):
            def half_of(group):
                return slice(half(group) * TPG, (half(group) + 1) * TPG)

            def load_residual(group):
                sp.wait_ge(stored[half(group)], value(lambda g: 16 * (g // 2), group))
                stand_alone(sp)
                sp.dma_start(x1[:, half_of(group), :], tokens(x, group)).then_inc(
                    res_in[half(group)], 16)

            def spread_rows(group):
                read(sp, "gT", 0, group)
                stand_alone(sp)
                wait(sp, g_all_done, value(lambda g: g * E, group))
                for r in range(E // EG):
                    sp.dma_start(g_rows[32 * r:32 * r + 1, :, :], g_chan[EG * r:EG * (r + 1), :]).then_inc(
                        g_rows_in, 16)

            def store(group):
                sp.wait_ge(down_read, credited(2, 1, group))
                stand_alone(sp)
                sp.dma_start(tokens(out, group), x1[:, half_of(group), :]).then_inc(
                    stored[half(group)], 16)

            sp.dma_start(mask_c[:], masks).then_inc(mask_in, 16)
            for c in range(NWC):
                if c == 1:
                    sp.dma_start(row_c[:], rows.partition_broadcast(P)).then_inc(consts_in, 16)
                    sp.dma_start(col_c[:], columns).then_inc(consts_in, 16)
                if c >= STAGE:
                    sp.wait_ge(w_lo_done, c - STAGE + 1)
                sp.dma_start(stage[:, c % STAGE, :], weights[:, c * WCHUNK:(c + 1) * WCHUNK]).then_inc(
                    w_in[c % STAGE], 16)
            sp.wait_ge(w_lo_done, NWC)
            with sp.Fori(0, ITER) as i:
                spread_rows((i, 0))
                spread_rows((i, 1))
                store((i, 0))
                load_residual((i, 2))
                store((i, 1))
                load_residual((i, 3))
            spread_rows(GROUPS - 2)
            spread_rows(GROUPS - 1)
            store(GROUPS - 2)
            store(GROUPS - 1)
            for k in range(2):
                sp.wait_ge(stored[k], 16 * SEQS)

        @block.tensor
        def _(pe):
            def take(step, j, group):
                bank, n = fill(step, j, group)
                wait(pe, bank_read[bank], n - 1)
                return att[:, bank, :], bank_full[bank]

            def product(dst, w_at, w_n, a_hi, a_lo, tokens_stationary):
                n = 0
                for w, a in ((w_hi, a_hi), (w_lo, a_hi), (w_hi, a_lo)):
                    for k in range(KC):
                        wk = w[:, w_at(k):w_at(k) + w_n]
                        lhs, rhs = (a(k), wk) if tokens_stationary else (wk, a(k))
                        mm = pe.matmul(dst, lhs, rhs, start=n == 0, stop=n == 3 * KC - 1)
                        n += 1
                return mm

            def turn(step, source, group):
                for c in range(KC):
                    dst, full = take(step, c, group)
                    for t in range(TPG):
                        mm = pe.transpose(dst[:, t * P:(t + 1) * P], source[:, t, c * P:(c + 1) * P], ident)
                    mm.then_inc(full, 1)

            def turn_back(step, j, source, at, group):
                dst, full = take(step, j, group)
                for t in range(2):
                    for c in range(KC):
                        mm = pe.transpose(dst[:, t * C + c * P:t * C + (c + 1) * P],
                                          source[:, c, at + t * P:at + (t + 1) * P], ident)
                mm.then_inc(full, 1)

            def x_turn(group):
                after(pe, "ln_x_norm", group)
                turn("xT", x_tok, group)

            def k_project(group):
                for c in range(KC):
                    read(pe, "xT", c, group)
                for c in range(KC):
                    dst, full = take("k", c, group)
                    hi, lo = x_turned(group)
                    product(dst, lambda k: QKV0 + k * 3 * C + 2 * C + c * P, P,
                            lambda k: hi[:, k, :], lambda k: lo[:, k, :], False).then_inc(full, 1)

            def tile_product(dst, w_at, w_n, hi, lo, t):
                cols = slice(t * P, (t + 1) * P)
                return product(dst, w_at, w_n, lambda k: hi[:, k, cols], lambda k: lo[:, k, cols], True)

            def project(step, w_at, w_n):
                def run(group):
                    hi, lo = (act_hi[:], act_lo[:]) if step == "wo" else x_turned(group)
                    for j in range(2):
                        dst, full = take(step, j, group)
                        for t in (2 * j, 2 * j + 1):
                            mm = tile_product(dst[:, (t % 2) * C:(t % 2 + 1) * C], w_at, w_n, hi, lo, t)
                        mm.then_inc(full, 1)
                return run

            def q_turn(group):
                after(pe, "softmax_mul", group)
                turn("qT", q_tok, group)

            def e_turn(i):
                def run(group):
                    after(pe, "k_exp", group)
                    turn_back(f"eT{i}", 0, k_chan, 2 * i * P, group)
                return run

            def state_sum(i):
                def run(group):
                    read(pe, f"eT{i}", 0, group)
                    if i == 0:
                        for c in range(KC):
                            take("st3", c, group)
                    for t in range(2):
                        for c in range(KC):
                            n = 2 * i + t
                            mm = pe.matmul(att[:, FILLS["st3"][c], 0:P],
                                           n_tok[:, 2 * (i % 2) + t, c * P:(c + 1) * P],
                                           v_tok[:, n, c * P:(c + 1) * P], start=n == 0, stop=n == TPS - 1)
                            if n == TPS - 1:
                                mm.then_inc(bank_full[FILLS["st3"][c]], 1)
                    if i < 2:
                        mm.then_inc(signal["st_part"], 1)
                return run

            def attend(group):
                seq_start = shift(group, -half(group))
                for c in range(KC):
                    read(pe, "st3", c, seq_start)
                read(pe, "qT", 1, group)
                g = half(group)
                for j in range(2):
                    dst, full = take("out", j, group)
                    for t in (2 * j, 2 * j + 1):
                        for c in range(KC):
                            at = g * GT + t * P
                            mm = pe.matmul(dst[:, (t % 2) * C + c * P:(t % 2) * C + (c + 1) * P],
                                           q_chan[:, c, at:at + P], state[:, c, :], start=True, stop=True)
                    mm.then_inc(full, 1)

            def o_turn(group):
                for j in range(2):
                    read(pe, "out", j, group)
                turn("oT", n_tok, group)

            def o_project(group):
                after(pe, "oT_lo", group)
                project("wo", lambda k: WO0 + k * C, C)(group)

            def f_turn(group):
                after(pe, "ln_f_norm", group)
                turn("fT", n_tok, group)

            def gate(group):
                for c in range(KC):
                    read(pe, "fT", c, group)
                pe.wait_ge(gate_parts_done, 2)
                dst, full = take("gate", 0, group)
                g = half(group)
                for t in range(TPG):
                    parts = [(part, k) for part in (f_hi, f_lo) for k in range(KC)]
                    for n, (part, k) in enumerate(parts):
                        mm = pe.matmul(dst[:, t * 2 * E:(t + 1) * 2 * E], part[:, g, k, t * P:(t + 1) * P],
                                       gate_parts[:, k].rearrange("p n e -> p (n e)"),
                                       start=n == 0, stop=n == len(parts) - 1)
                mm.then_inc(full, 1)

            def g_turn(group):
                after(pe, "route_weight", group)
                dst, full = take("gT", 0, group)
                for t in range(TPG):
                    mm = pe.transpose(dst[0:E, t * P:(t + 1) * P], r_root[:, 3, t, :], ident)
                mm.then_inc(full, 1)

            def consts(_):
                pe.wait_ge(consts_in, 32)

            mine = {
                "consts": consts,
                "xT": x_turn, "k": k_project, "q": project("q", lambda k: QKV0 + k * 3 * C, C),
                "v": project("v", lambda k: QKV0 + k * 3 * C + C, C), "qT": q_turn,
                "eT0": e_turn(0), "eT1": e_turn(1), "eT2": e_turn(2), "eT3": e_turn(3),
                "st0": state_sum(0), "st1": state_sum(1), "st2": state_sum(2), "st3": state_sum(3),
                "out": attend, "oT": o_turn, "wo": o_project, "fT": f_turn, "gate": gate, "gT": g_turn,
                "w_ready": lambda n: pe.wait_ge(w_lo_done, n),
            }

            def up(j, group):
                g = half(group)
                if j == 0:
                    for c in range(KC):
                        read(pe, "fT", c, group)
                pe.wait_ge(y_rooted, credited(CH, j - 2, group))
                product(hid[:, j % 2, :], lambda k: UP0 + j * C + k * P, P,
                        lambda k: f_hi[:, g, k, :], lambda k: f_lo[:, g, k, :], False).then_inc(hid_done, 1)

            def down_product(j, group):
                at = DOWN0 + j * C
                pe.wait_ge(y_hi_done, counted(CH, j, group))
                for n, (w, part) in enumerate(((w_hi, y_hi), (w_lo, y_hi), (w_hi, y_lo))):
                    if n == 2:
                        pe.wait_ge(y_lo_done, credited(CH, j, group))
                    for t in range(TPG):
                        if j == 0 and n == 0 and t % 2 == 0:
                            pe.wait_ge(down_read, credited(2, t // 2 - 2, group))
                        mm = pe.matmul(down[:, t // 2, (t % 2) * C:(t % 2 + 1) * C],
                                       part[:, j % HB, t * P:(t + 1) * P], w[:, at:at + C],
                                       start=j == 0 and n == 0 and t % 2 == 0, stop=j == CH - 1 and n == 2,
                                       skip_group_check=True)
                mm.then_inc(y_used, 1)

            def sequence(i, slots):
                for s in range(2 * CH + LAG):
                    if s < 2 * CH:
                        up(*chunk(s, i))
                    if s >= LAG:
                        down_product(*chunk(s - LAG, i))
                    steps_at(slots, s, i, mine)

            pe.sem_inc(y_used, CH)
            pe.wait_ge(mask_in, 16)
            for name, g in PROLOGUE:
                if name in mine:
                    mine[name](g)
            pe.wait_ge(w_lo_done, NWC)
            with pe.Fori(0, ITER) as i:
                sequence(i, SLOTS)
            sequence(ITER, without_next(SLOTS))

        @block.scalar
        def _(act):
            def load_x(group):
                bank, n = fill("xT", KC - 1, shift(group, -1))
                act.wait_ge(bank_full[bank], n)
                act.dma_start(x_tok[:], tokens(x, group)).then_inc(x_in, 16)

            def ln_apply(n):
                def run(group):
                    k = norm_place(n, group)
                    if (n, group) == ("x", 1):
                        all_used(act, ("xT",), "ln_x_apply", group)
                    after(act, f"ln_{n}_apply", group)
                    for t in range(TPG):
                        if n == "o":
                            src = att[:, FILLS["out"][t // 2], (t % 2) * C:(t % 2 + 1) * C]
                        else:
                            src = (raw_x(group) if n == "x"
                                   else x1[:, half(group) * TPG:(half(group) + 1) * TPG])[:, t, :]
                        last = nc.scalar.activation((x_tok if n == "x" else n_tok)[:, t, :], src, ACT.Identity,
                                                    scale=root[:, k, 2, t:t + 1], bias=root[:, k, 0, t:t + 1])
                        if n == "o" and t % 2:
                            last.then_inc(reader_of("out", t // 2), 1)
                    if n != "o":
                        last.then_inc(signal[f"ln_{n}_norm"], 1)
                return run

            def ln_root(n):
                def run(group):
                    step, k = f"ln_{n}_root", norm_place(n, group)
                    after(act, f"ln_{n}_stats", group)
                    nc.scalar.activation(root[:, k, 0, :], root[:, k, 3, :], ACT.Ln).then_inc(signal[step], 1)
                    after(act, step, group, 1)
                    nc.scalar.activation(root[:, k, 1, :], root[:, k, 0, :], ACT.Exp, scale=-0.5).then_inc(
                        signal[step], 1)
                return run

            def x_hi(group):
                if group != 1:
                    all_used(act, PROJECTIONS, "xT", group)
                for c in range(KC):
                    src = filled(act, "xT", c, group)
                    nc.scalar.activation(x_turned(group)[0][:, c, :], src, ACT.Copy).then_inc(signal["xT_hi"], 1)

            def k_out(group):
                all_used(act, ("eT3",), "k", group)
                g = half(group)
                for c in range(KC):
                    src = filled(act, "k", c, group)
                    nc.scalar.activation(k_chan[:, c, g * GT:(g + 1) * GT], src, ACT.Identity,
                                         bias=b_k[:, c:c + 1]).then_inc(reader_of("k", c), 1)

            def q_exponent(group):
                after(act, "softmax_sub", group)
                nc.scalar.activation(q_tok[:], q_tok[:], ACT.Exp).then_inc(signal["softmax_exp"], 1)

            def q_out(group):
                all_used(act, ("out",), "qT", group)
                g = half(group)
                for c in range(KC):
                    src = filled(act, "qT", c, group)
                    nc.scalar.activation(q_chan[:, c, g * GT:(g + 1) * GT], src, ACT.Copy).then_inc(
                        reader_of("qT", c), 1)

            def k_exponent(group):
                after(act, "k_max", group)
                for c in range(KC):
                    nc.scalar.activation(k_chan[:, c, :], k_chan[:, c, :], ACT.Exp, bias=kneg[:, 1, c:c + 1],
                                         accum_out=ksum[:, 0, c:c + 1]).then_inc(signal["k_exp"], 1)

            def e_out(i):
                def run(group):
                    if i == 0:
                        all_used(act, ("fT",), "eT0", group)
                    if i >= 2:
                        after(act, "st_part", group, i - 1)
                    src = filled(act, f"eT{i}", 0, group)
                    h = 2 * (i % 2)
                    nc.scalar.activation(n_tok[:, h:h + 2, :].rearrange("p t c -> p (t c)"), src,
                                         ACT.Copy).then_inc(reader_of(f"eT{i}", 0), 1)
                return run

            def o_scale(group):
                all_used(act, PROJECTIONS, "oT", group)
                for c in range(KC):
                    src = filled(act, "oT", c, group)
                    nc.scalar.activation(o_chan[:, c, :], src, ACT.Identity, bias=ln_b[:, c:c + 1],
                                         scale=ln_g[:, c:c + 1]).then_inc(reader_of("oT", c), 1)
                for c in range(KC):
                    read(act, "oT", c, group)
                    nc.scalar.activation(act_hi[:, c, :], o_chan[:, c, :], ACT.Copy).then_inc(signal["oT_hi"], 1)

            def f_split(group):
                wait(act, hid_done, value(lambda g: (g - 1) * CH, group))
                g = half(group)
                for c in range(KC):
                    src = filled(act, "fT", c, group)
                    nc.scalar.activation(f_hi[:, g, c, :], src, ACT.Copy).then_inc(signal["fT_hi"], 1)

            def gate_exp(group):
                read(act, "gate", 0, group)
                nc.scalar.activation(r_pick[:], r_score[:], ACT.Exp, scale=-1.0).then_inc(
                    signal["gate_exp"], 1)

            def route_root(group):
                after(act, "route_pick", group)
                nc.scalar.activation(r_root[:, 2, :, :], r_root[:, 1, :, :], ACT.Ln).then_inc(signal["route_root"], 1)
                after(act, "route_root", group, 1)
                nc.scalar.activation(r_root[:, 2, :, :], r_root[:, 2, :, :], ACT.Exp, scale=0.5).then_inc(
                    signal["route_root"], 1)

            def g_out(group):
                wait(act, g_rows_in, value(lambda g: g * 16 * (E // EG), group))
                src = filled(act, "gT", 0, group)
                nc.scalar.activation(g_chan[:], src[0:E, :], ACT.Copy).then_inc(reader_of("gT", 0), 1)

            def consts(_):
                act.wait_ge(consts_in, 32)
                nc.scalar.activation(gate_parts[:, :, 0, :], gate_w.rearrange("p (k e) -> p k e", e=E),
                                     ACT.Copy).then_inc(gate_parts_done, 1)

            mine = {
                "consts": consts,
                **{f"ln_{n}_root": ln_root(n) for n in LN}, **{f"ln_{n}_apply": ln_apply(n) for n in LN},
                "load_x": load_x, "xT": x_hi, "k": k_out, "softmax_exp": q_exponent,
                "qT": q_out, "k_exp": k_exponent, "eT0": e_out(0), "eT1": e_out(1), "eT2": e_out(2),
                "eT3": e_out(3), "oT": o_scale, "fT": f_split, "gate": gate_exp, "route_root": route_root,
                "gT": g_out,
            }

            def square(j, group):
                act.wait_ge(y_rooted, credited(CH, j, group))
                nc.scalar.activation(y[:, j % YB, :], y[:, j % YB, :], ACT.Square).then_inc(y_squared, 1)
                act.wait_ge(y_squared, counted(CH, j, group))
                act.wait_ge(y_used, credited(CH, j - HB, group))
                nc.scalar.activation(y_hi[:, j % HB, :], y[:, j % YB, :], ACT.Copy).then_inc(y_hi_done, 1)

            def sequence(i, slots):
                for s in range(2 * CH + LAG):
                    if s < 2 * CH:
                        square(*chunk(s, i))
                    steps_at(slots, s, i, mine)

            def split_weights(c):
                act.wait_ge(w_in[c % STAGE], 16 * (c // STAGE + 1))
                nc.scalar.activation(w_hi[:, c * WCHUNK:(c + 1) * WCHUNK], stage[:, c % STAGE, :],
                                     ACT.Copy).then_inc(w_hi_done, 1)

            mine["split"] = split_weights

            act.dma_start(x1[:, 0:TPG, :], tokens(x, 0)).then_inc(res_in[0], 16)
            act.dma_start(x1[:, TPG:TPS, :], tokens(x, 1)).then_inc(res_in[1], 16)
            nc.scalar.preload_act_table_set("natural_log_exp_and_others")
            act.sem_inc(down_read, 2)
            for name, g in PROLOGUE:
                if name in mine:
                    mine[name](g)
            with act.Fori(0, ITER) as i:
                sequence(i, SLOTS)
            sequence(ITER, without_next(SLOTS))

        @block.vector
        def _(dve):
            v = nc.vector

            class Run:

                def __init__(self, step, group):
                    self.step, self.group, self.n = step, group, 0

                def did(self, instruction):
                    instruction.then_inc(signal[self.step], 1)
                    self.n += 1

                def settle(self):
                    after(dve, self.step, self.group, self.n)

                def then(self, instruction):
                    self.did(instruction)
                    self.settle()

                def end(self):
                    assert self.n == SIGNALS[self.step], (self.step, self.n)

            def ln_stats(n):
                def run(group):
                    k, r, g = norm_place(n, group), Run(f"ln_{n}_stats", group), half(group)
                    if n == "x" and isinstance(group, int) and group < 2:
                        dve.wait_ge(res_in[group], 16)
                    elif n == "x":
                        dve.wait_ge(x_in, value(lambda q: 16 * (q - 1), group))
                    for t in range(TPG):
                        if n == "x":
                            src = raw_x(group)[:, t, :]
                        elif n == "o":
                            if t % 2 == 0:
                                bank = filled(dve, "out", t // 2, group)
                            src = bank[:, (t % 2) * C:(t % 2 + 1) * C]
                        else:
                            if t == 0:
                                for j in range(2):
                                    read(dve, "wo", j, group)
                            src = x1[:, g * TPG + t, :]
                        last = v.bn_stats(stats[:, k, t, :], src)
                    r.then(last)
                    stand_alone(dve)
                    for t in range(TPG):
                        last = v.bn_aggr(mv[:, k, t, :], stats[:, k, t, :])
                    r.then(last)
                    r.did(v.tensor_scalar(root[:, k, 3, :], mv[:, k, :, 1], EPS, None, ALU.add))
                    r.end()
                return run

            def ln_apply(n):
                def run(group):
                    k, r, g = norm_place(n, group), Run(f"ln_{n}_apply", group), half(group)
                    after(dve, f"ln_{n}_root", group)
                    r.then(v.tensor_tensor(root[:, k, 2, :], root[:, k, 1, :], root[:, k, 1, :], ALU.mult))
                    r.then(v.scalar_tensor_tensor(out=root[:, k, 2, :], in0=root[:, k, 2, :], scalar=-0.5,
                                                  in1=root[:, k, 3, :], op0=ALU.mult, op1=ALU.mult))
                    r.then(v.scalar_tensor_tensor(out=root[:, k, 2, :], in0=root[:, k, 2, :], scalar=1.5,
                                                  in1=root[:, k, 1, :], op0=ALU.add, op1=ALU.mult))
                    r.did(v.scalar_tensor_tensor(out=root[:, k, 0, :], in0=mv[:, k, :, 0], scalar=-1.0,
                                                 in1=root[:, k, 2, :], op0=ALU.mult, op1=ALU.mult))
                    r.end()
                return run

            def x_lo(group):
                hi, lo = x_turned(group)
                for c in range(KC):
                    after(dve, "xT_hi", group, c + 1)
                    v.tensor_tensor(lo[:, c, :], att[:, FILLS["xT"][c], :], hi[:, c, :].bitcast(F32),
                                    ALU.subtract).then_inc(reader_of("xT", c), 1)

            def k_top(group):
                r = Run("k_top", group)
                g = half(group)
                for c in range(KC):
                    read(dve, "k", c, group)
                    r.did(v.tensor_reduce(kmax[:, c, g:g + 1], k_chan[:, c, g * GT:(g + 1) * GT], AX.X, ALU.max))
                r.end()

            def bias_add(step, target, bias, last_user):
                def run(group):
                    all_used(dve, (last_user,), step, group)
                    at = half(group) * TPG if step == "v" else 0
                    for j in range(2):
                        src = filled(dve, step, j, group)
                        v.tensor_tensor(target[:, at + 2 * j:at + 2 * j + 2, :],
                                        src.rearrange("p (t c) -> p t c", c=C),
                                        bias.unsqueeze(1).broadcast_to([P, 2, C]), ALU.add).then_inc(
                            reader_of(step, j), 1)
                return run

            def softmax_max(group):
                r = Run("softmax_max", group)
                for j in range(2):
                    read(dve, "q", j, group)
                r.did(v.tensor_reduce(qmax[:], q_tok[:].rearrange("p t (h d) -> p (t h) d", d=HD), AX.X, ALU.max))
                r.end()

            def softmax_sum(group):
                r = Run("softmax_sum", group)
                after(dve, "softmax_exp", group)
                r.then(v.tensor_reduce(qsum[:, 0, :], q_tok[:].rearrange("p t (h d) -> p (t h) d", d=HD),
                                       AX.X, ALU.add))
                r.did(v.reciprocal(qsum[:, 1, :], qsum[:, 0, :]))
                r.end()

            def k_max(group):
                r = Run("k_max", group)
                after(dve, "k_top", shift(group, 1))
                r.then(v.tensor_tensor(kneg[:, 0, :], kmax[:, :, 0], kmax[:, :, 1], ALU.max))
                r.did(v.tensor_scalar(kneg[:, 1, :], kneg[:, 0, :], -1.0, None, ALU.mult))
                r.end()

            def k_sum(group):
                r = Run("k_sum", group)
                after(dve, "k_exp", group)
                r.did(v.reciprocal(ksum[:, 1, :], ksum[:, 0, :]))
                r.end()

            def state_out(group):
                all_used(dve, ("out",), "state", group)
                after(dve, "k_sum", group)
                for c in range(KC):
                    src = filled(dve, "st3", c, group)
                    v.scalar_tensor_tensor(out=state[:, c, :], in0=src[:, 0:P], scalar=ksum[:, 1, c:c + 1],
                                           in1=same_head, op0=ALU.mult, op1=ALU.mult).then_inc(
                        reader_of("st3", c), 1)

            def o_lo(group):
                r = Run("oT_lo", group)
                for c in range(KC):
                    after(dve, "oT_hi", group, c + 1)
                    r.did(v.tensor_tensor(act_lo[:, c, :], o_chan[:, c, :], act_hi[:, c, :].bitcast(F32),
                                          ALU.subtract))
                r.end()

            def residual_add(group):
                after(dve, "residual", group)
                for j in range(2):
                    src = filled(dve, "wo", j, group)
                    at = half(group) * TPG + 2 * j
                    part = x1[:, at:at + 2, :].rearrange("p t c -> p (t c)")
                    v.tensor_tensor(part, src, part, ALU.add).then_inc(reader_of("wo", j), 1)

            def f_lo_out(group):
                for c in range(KC):
                    after(dve, "fT_hi", group, c + 1)
                    v.tensor_tensor(f_lo[:, half(group), c, :], att[:, FILLS["fT"][c], :],
                                    f_hi[:, half(group), c, :].bitcast(F32), ALU.subtract).then_inc(
                        reader_of("fT", c), 1)

            def logits(group):
                r = Run("logits", group)
                src = filled(dve, "gate", 0, group)[:, 0:TPG * 2 * E].rearrange("p (t n e) -> p t n e", n=2, e=E)
                r.then(v.tensor_copy(r_score[:], src[:, :, 0, :]))
                v.tensor_tensor(r_score[:], r_score[:], src[:, :, 1, :], ALU.add).then_inc(
                    reader_of("gate", 0), 1)
                r.end()

            def route_group(group):
                r = Run("route_group", group)
                after(dve, "gate_exp", group)
                scores = r_list[:, :, 0:E]
                by_group = scores.rearrange("p t (g e) -> p t g e", e=EG)
                pairs = r_half[:].rearrange("p h (t g) e -> p h t g e", g=EG)
                r.then(v.tensor_scalar(r_pick[:], r_pick[:], 1.0, None, ALU.add))
                r.then(v.reciprocal(r_score[:], r_pick[:]))
                r.then(v.tensor_tensor(scores, r_score[:], b_e.unsqueeze(1).broadcast_to([P, TPG, E]), ALU.add))
                r.did(v.tensor_tensor(pairs[:, 0], by_group[:, :, :, 0::2], by_group[:, :, :, 1::2], ALU.max))
                r.then(v.tensor_tensor(pairs[:, 1], by_group[:, :, :, 0::2], by_group[:, :, :, 1::2], ALU.min))
                r.did(v.tensor_tensor(r_pair[:, :, 0:2], r_half[:, 0], r_half[:, 1], ALU.add))
                r.then(v.tensor_tensor(r_pair[:, :, 2], r_half[:, 0, :, 0], r_half[:, 0, :, 1], ALU.add))
                best = r_group[:, 0]
                r.then(v.tensor_reduce(best.rearrange("p t g -> p (t g)"), r_pair[:], AX.X, ALU.max))
                other = best.unsqueeze(2).broadcast_to([P, TPG, EG, EG])
                own = best.unsqueeze(3).broadcast_to([P, TPG, EG, EG])
                above = r_above[:].rearrange("p n (t g) o -> p n t g o", g=EG)
                r.did(v.tensor_tensor(above[:, 0], other, own, ALU.is_gt))
                r.then(v.tensor_tensor(above[:, 1], other, own, ALU.is_equal))
                flat_above = r_above[:].rearrange("p n (t g) o -> p n t (g o)", g=EG)
                r.then(v.tensor_tensor(flat_above[:, 1], flat_above[:, 1],
                                       earlier.unsqueeze(1).broadcast_to([P, TPG, EG * EG]), ALU.mult))
                r.then(v.tensor_tensor(r_above[:, 0], r_above[:, 0], r_above[:, 1], ALU.add))
                keep = r_group[:, 1]
                r.then(v.tensor_reduce(keep.rearrange("p t g -> p (t g)"), r_above[:, 0], AX.X, ALU.add))
                r.then(v.tensor_scalar(keep, keep, 1.5, None, ALU.is_lt))
                r.did(v.tensor_tensor(by_group, by_group, keep.unsqueeze(3).broadcast_to([P, TPG, EG, EG]),
                                      ALU.mult))
                r.end()

            def route_pick(group):
                r = Run("route_pick", group)
                after(dve, "route_group", group)
                stand_alone(dve)
                for t in range(TPG):
                    last = v.max(r_best[:, t, :], r_list[:, t, 0:E])
                r.then(last)
                r.then(v.memset(r_best[:, :, 4:8], NONE))
                stand_alone(dve)
                for t in range(TPG):
                    last = v.match_replace(r_left[:, t, :], r_best[:, t, :], r_list[:, t, :], -NONE)
                r.then(last)
                r.then(v.tensor_scalar(r_pick[:], r_left[:, :, 0:E], -NONE, None, ALU.is_equal))
                r.then(v.tensor_tensor(r_root[:, 0], r_score[:], r_pick[:], ALU.mult))
                r.then(v.tensor_reduce(r_sum[:, 0, :], r_root[:, 0], AX.X, ALU.add))
                r.then(v.tensor_scalar(r_sum[:, 0, :], r_sum[:, 0, :], 1e-20, None, ALU.add))
                r.then(v.reciprocal(r_sum[:, 1, :], r_sum[:, 0, :]))
                r.then(v.scalar_tensor_tensor(out=r_root[:, 0], in0=r_root[:, 0], scalar=2.5,
                                              in1=r_sum[:, 1, :].unsqueeze(2).broadcast_to([P, TPG, E]),
                                              op0=ALU.mult, op1=ALU.mult))
                r.did(v.tensor_scalar(r_root[:, 1], r_root[:, 0], 1e-18, None, ALU.max))
                r.end()

            def route_weight(group):
                r = Run("route_weight", group)
                after(dve, "route_root", group)
                r.then(v.reciprocal(r_root[:, 1], r_root[:, 2]))
                r.then(v.tensor_tensor(r_root[:, 1], r_root[:, 0], r_root[:, 1], ALU.mult))
                r.then(v.tensor_tensor(r_root[:, 1], r_root[:, 1], r_root[:, 2], ALU.add))
                r.did(v.scalar_tensor_tensor(out=r_root[:, 3], in0=r_root[:, 1], scalar=0.5, in1=r_pick[:],
                                             op0=ALU.mult, op1=ALU.mult))
                r.end()

            def ffn_add(group):
                dve.wait_ge(y_used, credited(CH, CH - 1, group))
                for j in range(2):
                    src = down[:, j, :]
                    at = half(group) * TPG + 2 * j
                    part = x1[:, at:at + 2, :].rearrange("p t c -> p (t c)")
                    v.tensor_tensor(part, src, part, ALU.add).then_inc(down_read, 1)

            def consts(_):
                dve.wait_ge(consts_in, 32)
                dve.wait_ge(mask_in, 16)
                dve.wait_ge(gate_parts_done, 1)
                v.tensor_tensor(gate_parts[:, :, 1, :], gate_w.rearrange("p (k e) -> p k e", e=E),
                                gate_parts[:, :, 0, :].bitcast(F32), ALU.subtract).then_inc(gate_parts_done, 1)

            mine = {
                "consts": consts,
                **{f"ln_{n}_stats": ln_stats(n) for n in LN}, **{f"ln_{n}_apply": ln_apply(n) for n in LN},
                "xT": x_lo, "k": k_top, "q": bias_add("q", q_tok, b_qv[:, 0:C], "qT"), "v": bias_add("v", v_tok, b_qv[:, C:2 * C], "st3"),
                "softmax_max": softmax_max, "softmax_sum": softmax_sum, "k_max": k_max, "k_sum": k_sum,
                "state": state_out, "oT": o_lo, "wo": residual_add, "fT": f_lo_out,
                "gate": logits, "route_group": route_group, "route_pick": route_pick, "route_weight": route_weight, "ffn_out": ffn_add,
            }

            def weigh(j, group):
                dve.wait_ge(hid_done, counted(CH, j, group))
                last = j - YB if j >= YB else max(n for n in range(CH) if n % YB == j) - CH
                dve.wait_ge(y_lo_done, credited(CH, last, group))
                if j >= SH:
                    dve.wait_ge(g_all_done, counted(E, j - SH, group))
                    v.scalar_tensor_tensor(out=y[:, j % YB, :], in0=hid[:, j % 2, :], scalar=0.0,
                                           in1=g_all[:, (j - SH) % GB, :], op0=ALU.max, op1=ALU.mult).then_inc(y_rooted, 1)
                else:
                    v.tensor_scalar(y[:, j % YB, :], hid[:, j % 2, :], 0.0, None, ALU.max).then_inc(y_rooted, 1)

            def split(j, group):
                dve.wait_ge(y_hi_done, counted(CH, j, group))
                v.tensor_tensor(y_lo[:, j % HB, :], y[:, j % YB, :], y_hi[:, j % HB, :].bitcast(F32),
                                ALU.subtract).then_inc(y_lo_done, 1)

            def sequence(i, slots):
                for s in range(2 * CH + LAG):
                    if s < 2 * CH:
                        weigh(*chunk(s, i))
                    if 1 <= s <= 2 * CH:
                        split(*chunk(s - 1, i))
                    steps_at(slots, s, i, mine)

            def split_weights(c):
                dve.wait_ge(w_hi_done, c + 1)
                at = slice(c * WCHUNK, (c + 1) * WCHUNK)
                v.tensor_tensor(w_lo[:, at], stage[:, c % STAGE, :], w_hi[:, at].bitcast(F32),
                                ALU.subtract).then_inc(w_lo_done, 1)

            mine["split"] = split_weights

            dve.sem_inc(y_rooted, CH)
            dve.sem_inc(y_lo_done, CH)
            v.memset(r_list[:, :, E:E + 4], NONE).then_inc(list_end, 1)
            dve.wait_ge(list_end, 1)
            for name, g in PROLOGUE:
                if name in mine:
                    mine[name](g)
            with dve.Fori(0, ITER) as i:
                sequence(i, SLOTS)
            sequence(ITER, without_next(SLOTS))

        @block.gpsimd
        def _(pool):
            def softmax_sub(group):
                after(pool, "softmax_max", group)
                heads = q_tok[:].rearrange("p t (h d) -> p (t h) d", d=HD)
                nc.gpsimd.tensor_tensor(heads, heads, qmax[:].unsqueeze(2).broadcast_to([P, TPG * HEADS, HD]),
                                        ALU.subtract).then_inc(signal["softmax_sub"], 1)
                after(pool, "softmax_sub", group)

            def softmax_mul(group):
                after(pool, "softmax_sum", group)
                heads = q_tok[:].rearrange("p t (h d) -> p (t h) d", d=HD)
                nc.gpsimd.tensor_tensor(heads, heads, qsum[:, 1, :].unsqueeze(2).broadcast_to([P, TPG * HEADS, HD]),
                                        ALU.mult).then_inc(signal["softmax_mul"], 1)
                after(pool, "softmax_mul", group)

            def residual(group):
                after(pool, "ln_x_norm", group)
                stand_alone(pool)
                pool.wait_ge(res_in[half(group)], value(lambda g: 16 * (g // 2 + 1), group))
                at = half(group) * TPG
                part = x1[:, at:at + TPG, :]
                nc.gpsimd.tensor_tensor(part, part, b_o.unsqueeze(1).broadcast_to([P, TPG, C]),
                                        ALU.add).then_inc(signal["residual"], 1)
                after(pool, "residual", group)

            def consts(_):
                pool.wait_ge(consts_in, 32)

            mine = {"consts": consts, "softmax_sub": softmax_sub, "softmax_mul": softmax_mul, "residual": residual}

            def broadcast(e, group):
                if e == 0:
                    pool.wait_ge(g_rows_in, value(lambda g: 16 * (E // EG) * (g + 1), group))
                pool.wait_ge(y_rooted, credited(CH, e - GB + SH if e >= GB else e - GB, group))
                stand_alone(pool)
                row = 32 * (e // EG)
                nc.gpsimd.partition_broadcast(g_all[:, e % GB, :], g_rows[row:row + 1, e % EG, :], P).then_inc(
                    g_all_done, 1)
                pool.wait_ge(g_all_done, counted(E, e, group))
                stand_alone(pool)

            def sequence(i, slots):
                for s in range(2 * CH + LAG):
                    if s < 2 * CH and s % CH >= SH:
                        j, group = chunk(s, i)
                        broadcast(j - SH, group)
                    steps_at(slots, s, i, mine)

            for name, g in PROLOGUE:
                if name in mine:
                    mine[name](g)
            with pool.Fori(0, ITER) as i:
                sequence(i, SLOTS)
            sequence(ITER, without_next(SLOTS))


def kernel(L0_attn_x, L0_attn_Wq, L0_attn_bq, L0_attn_Wk, L0_attn_bk, L0_attn_Wv, L0_attn_bv, L0_attn_Wo,
           L0_attn_bo, L0_attn_ln_g, L0_attn_ln_b, L0_ffn_gate_w, L0_ffn_bias_e, L0_ffn_up_w, L0_ffn_down_w,
           L0_ffn_shared_up, L0_ffn_shared_down):
    import numpy as np
    import concourse.bacc as bacc
    from concourse.bass_utils import run_bass_kernel_spmd

    B, N, C = L0_attn_x.shape
    halves = C // P

    def by_channel(w):
        return np.asarray(w).T.reshape(halves, P, -1).transpose(1, 0, 2)

    qvk = np.concatenate([by_channel(L0_attn_Wq), by_channel(L0_attn_Wv), by_channel(L0_attn_Wk)], axis=2)
    ups = np.concatenate([np.asarray(L0_ffn_shared_up), np.asarray(L0_ffn_up_w).reshape(-1, C)], axis=0)
    chunks = ups.shape[0] // P
    ups = ups.reshape(chunks, P, halves, P).transpose(3, 0, 2, 1)
    downs = np.concatenate([np.asarray(L0_ffn_shared_down).reshape(C, -1, P).transpose(1, 0, 2),
                            np.asarray(L0_ffn_down_w)], axis=0)
    downs = downs.transpose(2, 0, 1)
    weights = np.concatenate([a.reshape(P, -1) for a in (qvk, by_channel(L0_attn_Wo), ups, downs)], axis=1)
    rows = np.concatenate([np.asarray(a) for a in (L0_attn_bq, L0_attn_bv, L0_attn_bo, L0_ffn_bias_e)])
    columns = np.concatenate([np.asarray(a).reshape(halves, P).T for a in (L0_attn_bk, L0_attn_ln_g, L0_attn_ln_b)]
                             + [by_channel(L0_ffn_gate_w).reshape(P, -1)], axis=1)
    head = np.arange(P) // 16
    earlier = (np.arange(4)[None, :] < np.arange(4)[:, None]).reshape(1, -1).repeat(P, axis=0)
    masks = np.concatenate([np.eye(P), head[:, None] == head[None, :], earlier], axis=1).astype(np.float32)

    arrays = {"x": np.asarray(L0_attn_x).reshape(B * N, C), "weights": weights, "rows": rows,
              "columns": columns, "masks": masks}
    arrays = {k: np.ascontiguousarray(a) for k, a in arrays.items()}
    nc = bacc.Bacc("TRN2", target_bir_lowering=False, num_devices=1)
    ins = [nc.dram_tensor(k, a.shape, F32, kind="ExternalInput").ap() for k, a in arrays.items()]
    out = nc.dram_tensor("out", (B * N, C), F32, kind="ExternalOutput").ap()
    layer_kernel(nc, *ins, out)
    result = run_bass_kernel_spmd(nc, [arrays], core_ids=[0])
    return result.results[0]["out"].reshape(B, N, C)
```

```python
from contextlib import ExitStack

import concourse.bass as bass
from concourse import mybir

F32 = mybir.dt.float32
F32R = mybir.dt.float32r
ALU = mybir.AluOpType
ACT = mybir.ActivationFunctionType
AX = mybir.AxisListType

P = 128
EPS = 1e-5
TPG = 4
GT = TPG * P
BANK = 512
LAG = 2
WCHUNK = 512
STAGE = 7

FILLS = {
    "xT": (1, 0), "k": (3, 1), "q": (3, 1), "v": (3, 2), "qT": (1, 0), "eT0": (0,), "eT1": (1,),
    "eT2": (0,), "eT3": (1,), "st3": (2, 3), "out": (0, 2), "oT": (2, 3), "wo": (1, 0), "fT": (0, 3),
    "gate": (3,), "gT": (3,),
}
SIGNALS = {
    "ln_x_stats": 3, "ln_o_stats": 3, "ln_f_stats": 3,
    "ln_x_root": 2, "ln_o_root": 2, "ln_f_root": 2,
    "ln_x_apply": 4, "ln_o_apply": 4, "ln_f_apply": 4,
    "ln_x_norm": 1, "ln_f_norm": 1,
    "xT_hi": 2, "oT_hi": 2, "fT_hi": 2,
    "oT_lo": 2, "k_top": 2, "softmax_max": 1,
    "softmax_sub": 1, "softmax_mul": 1, "residual": 1,
    "softmax_exp": 1, "k_exp": 2,
    "softmax_sum": 2, "k_max": 2, "k_sum": 1,
    "st_part": 2,
    "route_group": 15, "route_pick": 10, "route_weight": 4,
    "logits": 1,
    "gate_exp": 1, "route_root": 2,
}
PROJECTIONS = ("k", "q", "v", "wo")
ONCE_A_SEQUENCE = {"k_exp", "k_max", "k_sum", "st_part"}

PROLOGUE = [
    ("ln_x_stats", 0), ("ln_x_stats", 1), ("split", 0), ("split", 1), ("split", 2), ("warm", 32),
    ("ln_x_root", 0), ("split", 3), ("ln_x_apply", 0), ("consts", 0), ("split", 4), ("ln_x_root", 1),
    ("xT", 0), ("ln_x_apply", 1), ("warm", 20), ("xT", 1), ("w_ready", 3), ("split", 5), ("split", 6),
    ("k", 0), ("residual", 0), ("k", 1), ("k_max", 0), ("k_exp", 0), ("q", 0), ("softmax_max", 0), ("v", 0),
    ("eT0", 0), ("v", 1), ("softmax_sub", 0), ("split", 7), ("softmax_exp", 0), ("eT1", 0), ("k_sum", 0),
    ("softmax_sum", 0), ("split", 8), ("st0", 0), ("softmax_mul", 0), ("split", 9), ("split", 10),
    ("w_ready", 4), ("split", 11), ("eT2", 0), ("st1", 0), ("eT3", 0), ("qT", 0), ("st2", 0), ("st3", 0),
    ("state", 0), ("out", 0), ("split", 12), ("split", 13), ("split", 14), ("ln_o_stats", 0), ("split", 15),
    ("q", 1), ("warm", 20), ("ln_o_root", 0), ("split", 16), ("ln_o_apply", 0), ("split", 17),
    ("split", 18), ("softmax_max", 1), ("softmax_sub", 1), ("warm", 18), ("oT", 0), ("softmax_exp", 1),
    ("softmax_sum", 1), ("split", 19), ("wo", 0), ("warm", 8), ("ln_f_stats", 0), ("split", 20),
    ("softmax_mul", 1), ("ln_f_root", 0), ("split", 21), ("ln_f_apply", 0), ("fT", 0), ("qT", 1),
    ("split", 22), ("gate", 0), ("route_group", 0), ("route_pick", 0), ("split", 23), ("route_root", 0),
    ("warm", 30), ("out", 1),
]
SLOTS = {
    0: [("load_x", 2), ("route_weight", 0)],
    1: [("gT", 0), ("ln_o_stats", 1), ("ln_o_root", 1)],
    2: [("ln_o_apply", 1)],
    4: [("ln_x_stats", 2), ("oT", 1)],
    5: [("ln_x_root", 2)],
    6: [("residual", 1), ("ln_x_apply", 2), ("wo", 1)],
    7: [("ln_f_stats", 1), ("xT", 2), ("ln_f_root", 1)],
    8: [("k", 2), ("ln_f_apply", 1), ("q", 2), ("softmax_max", 2)],
    9: [("fT", 1), ("load_x", 3)],
    10: [("ln_x_stats", 3), ("gate", 1)],
    11: [("ln_x_root", 3), ("softmax_sub", 2), ("softmax_exp", 2), ("route_group", 1)],
    12: [("v", 2)],
    13: [("route_pick", 1)],
    14: [("ln_x_apply", 3), ("route_root", 1)],
    15: [("softmax_sum", 2)],
    17: [("xT", 3), ("route_weight", 1)],
    18: [("softmax_mul", 2), ("qT", 2)],
    19: [("k", 3), ("k_max", 2)],
    20: [("q", 3), ("k_exp", 2)],
    21: [("eT0", 2), ("ffn_out", 0), ("gT", 1), ("softmax_max", 3)],
    23: [("v", 3)],
    24: [("st0", 2), ("eT2", 2), ("eT1", 2)],
    25: [("softmax_sub", 3), ("k_sum", 2), ("st1", 2), ("eT3", 2)],
    26: [("softmax_exp", 3), ("st2", 2)],
    27: [("softmax_sum", 3), ("residual", 2), ("st3", 2), ("state", 2)],
    28: [("out", 2), ("ln_o_stats", 2)],
    29: [("ln_o_root", 2), ("ln_o_apply", 2)],
    31: [("oT", 2)],
    32: [("softmax_mul", 3)],
    33: [("wo", 2), ("ln_f_stats", 2), ("ln_f_root", 2)],
    34: [("ln_f_apply", 2)],
    36: [("fT", 2)],
    37: [("gate", 2), ("qT", 3), ("route_group", 2)],
    39: [("out", 3)],
    40: [("route_pick", 2)],
    41: [("route_root", 2), ("ffn_out", 1)],
}


def without_next(slot):
    return {s: [x for x in steps if x[1] < 2] for s, steps in slot.items()}


def layer_kernel(nc, x, weights, rows, columns, masks, out):
    TOKENS, C = x.shape
    E, EG = 16, 4
    CH = weights.shape[1] // (2 * C) - 4
    SH = CH - E
    KC = C // P
    HD = 16
    HEADS = C // HD
    GROUPS = TOKENS // GT
    SEQS = GROUPS // 2
    TPS = 2 * TPG
    ITER = SEQS - 1
    NW = weights.shape[1]
    NWC = NW // WCHUNK
    QKV0, WO0, UP0 = 0, KC * 3 * C, KC * 4 * C
    DOWN0 = UP0 + CH * C
    NONE = -3.0e38

    def flat(i, slots):
        return [(n, g + 2 * i) for s in sorted(slots) for n, g in slots[s]]

    order = list(PROLOGUE)
    for i in range(ITER):
        order += flat(i, SLOTS)
    order += flat(ITER, without_next(SLOTS))
    place = {x: n for n, x in enumerate(order)}

    def value(f, group):
        if isinstance(group, tuple):
            i, g = group
            step = f(g + 2) - f(g)
            return i * step + f(g) if step else f(g)
        return f(group)

    def shift(group, by):
        return (group[0], group[1] + by) if isinstance(group, tuple) else group + by

    def half(group):
        return (group[1] if isinstance(group, tuple) else group) % 2

    def ahead(step, group, bank):
        return value(lambda g: sum(FILLS.get(s, ()).count(bank) for s, _ in order[:place[step, g]]), group)

    def fill(step, j, group):
        bank = FILLS[step][j]
        return bank, ahead(step, group, bank) + FILLS[step][:j + 1].count(bank)

    def wait(eng, sem, v):
        if not isinstance(v, int) or v > 0:
            eng.wait_ge(sem, v)

    with ExitStack() as ctx:
        def sb(name, shape, dt=F32):
            return ctx.enter_context(nc.sbuf_tensor(name, shape, dt))

        def sem(name):
            return ctx.enter_context(nc.semaphore(name))

        w_hi = sb("w_hi", [P, NW], F32R)
        w_lo = sb("w_lo", [P, NW], F32R)
        x_tok = sb("x_tok", [P, TPG, C])
        q_tok = sb("q_tok", [P, TPG, C])
        v_tok = sb("v_tok", [P, TPS, C])
        n_tok = sb("n_tok", [P, TPG, C])
        act_hi = sb("act_hi", [P, KC, GT], F32R)
        act_lo = sb("act_lo", [P, KC, GT], F32R)
        k_chan = sb("k_chan", [P, KC, 2 * GT])
        q_chan = sb("q_chan", [P, KC, 2 * GT])
        o_chan = sb("o_chan", [P, KC, GT])
        x1 = sb("x1", [P, TPS, C])
        f_hi = sb("f_hi", [P, 2, KC, GT], F32R)
        f_lo = sb("f_lo", [P, 2, KC, GT], F32R)
        g_chan = sb("g_chan", [E, GT])
        g_rows = sb("g_rows", [P, EG, GT])
        GB, YB, HB = 2, 3, 2
        g_all = sb("g_all", [P, GB, GT])
        y = sb("y", [P, YB, GT])
        y_hi = sb("y_hi", [P, HB, GT], F32R)
        y_lo = sb("y_lo", [P, HB, GT], F32R)
        gate_parts = sb("gate_parts", [P, KC, 2, E], F32R)
        state = sb("state", [P, KC, P])
        row_c = sb("row_c", [P, rows.shape[0]])
        col_c = sb("col_c", [P, columns.shape[1]])
        mask_c = sb("mask_c", [P, masks.shape[1]])
        LN = ("x", "o", "f")
        stats = sb("stats", [P, 3, TPG, 6])
        mv = sb("mv", [P, 3, TPG, 2])
        root = sb("root", [P, 3, 4, TPG])
        qmax = sb("qmax", [P, TPG * HEADS])
        qsum = sb("qsum", [P, 2, TPG * HEADS])
        kmax = sb("kmax", [P, KC, 2])
        kneg = sb("kneg", [P, 2, KC])
        ksum = sb("ksum", [P, 2, KC])
        r_score = sb("r_score", [P, TPG, E])
        r_pick = sb("r_pick", [P, TPG, E])
        r_half = sb("r_half", [P, 2, TPG * EG, 2])
        r_pair = sb("r_pair", [P, TPG * EG, 3])
        r_group = sb("r_group", [P, 2, TPG, EG])
        r_above = sb("r_above", [P, 2, TPG * EG, EG])
        r_list = sb("r_list", [P, TPG, E + 4])
        r_best = sb("r_best", [P, TPG, 8])
        r_left = sb("r_left", [P, TPG, E + 4])
        r_sum = sb("r_sum", [P, 2, TPG])
        r_root = sb("r_root", [P, 4, TPG, E])

        b_qv, b_o, b_e = row_c[:, 0:2 * C], row_c[:, 2 * C:3 * C], row_c[:, 3 * C:3 * C + E]
        b_k, ln_g, ln_b = col_c[:, 0:KC], col_c[:, KC:2 * KC], col_c[:, 2 * KC:3 * KC]
        gate_w = col_c[:, 3 * KC:3 * KC + KC * E]
        ident, same_head, earlier = mask_c[:, 0:P], mask_c[:, P:2 * P], mask_c[:, 2 * P:2 * P + EG * EG]
        stage = [g_rows[:, k, :] for k in range(EG)] + [y[:, k, :] for k in range(YB)]
        assert len(stage) == STAGE

        hid = ctx.enter_context(nc.psum_tensor("hid", [P, 2, BANK], F32))
        down = ctx.enter_context(nc.psum_tensor("down", [P, KC, BANK], F32))
        att = ctx.enter_context(nc.psum_tensor("att", [P, 4, BANK], F32))

        mask_in = sem("mask_in")
        columns_in = sem("columns_in")
        rows_in = sem("rows_in")
        w_in = [sem(f"w_in{k}") for k in range(STAGE)]
        w_hi_done = sem("w_hi_done")
        w_lo_done = [sem(f"w_lo_done{k}") for k in range(2)]
        x_in = sem("x_in")
        res_in = [sem(f"res_in{k}") for k in range(2)]
        stored = [sem(f"stored{k}") for k in range(2)]
        bank_full = [sem(f"bank_full{k}") for k in range(4)]
        bank_read = [sem(f"bank_read{k}") for k in range(4)]
        signal = {s: sem(s) for s in SIGNALS}
        g_rows_in = sem("g_rows_in")
        g_all_done = sem("g_all_done")
        gate_parts_done = sem("gate_parts_done")
        list_end = sem("list_end")
        hid_done = sem("hid_done")
        y_rooted = sem("y_rooted")
        y_squared = sem("y_squared")
        y_hi_done = sem("y_hi_done")
        y_lo_done = sem("y_lo_done")
        y_used = sem("y_used")
        down_read = sem("down_read")

        passed = {e: sem(f"passed_{e.name}") for e in (nc.sync.engine, nc.vector.engine, nc.gpsimd.engine)}

        def runs(step, group):
            per = SIGNALS[step]
            return value(lambda g: (g // 2 if step in ONCE_A_SEQUENCE else g) * per, group)

        def after(eng, step, group, k=None):
            eng.wait_ge(signal[step], runs(step, group) + (SIGNALS[step] if k is None else k))

        def filled(eng, step, j, group):
            bank, n = fill(step, j, group)
            eng.wait_ge(bank_full[bank], n)
            return att[:, bank, :]

        def read(eng, step, j, group):
            bank, n = fill(step, j, group)
            eng.wait_ge(bank_read[bank], n)

        def all_used(eng, users, step, group):
            for bank in sorted({FILLS[user][-1] for user in users}):
                wait(eng, bank_full[bank], ahead(step, group, bank))

        def reader_of(step, j):
            return bank_read[FILLS[step][j]]

        def credited(per_group, k, group):
            return value(lambda g: (g + 1) * per_group + k + 1, group)

        def counted(per_group, k, group):
            return value(lambda g: g * per_group + k + 1, group)

        def chunk(s, i):
            return s % CH, 2 * i + s // CH if isinstance(i, int) else (i, s // CH)

        def steps_at(slots, s, i, mine):
            for name, g in slots.get(s, ()):
                if name in mine:
                    mine[name](2 * i + g if isinstance(i, int) else (i, g))

        def stand_alone(eng):
            eng.sem_inc(passed[eng.engine], 1)

        def weights_split(eng, n):
            for k in range(2):
                wait(eng, w_lo_done[k], (n + 1 - k) // 2)

        def weights_lo(eng, ops, c):
            eng.wait_ge(w_hi_done, c + 1)
            at = slice(c * WCHUNK, (c + 1) * WCHUNK)
            ops.tensor_tensor(w_lo[:, at], stage[c % STAGE], w_hi[:, at].bitcast(F32),
                              ALU.subtract).then_inc(w_lo_done[c % 2], 1)

        def raw_x(group):
            if isinstance(group, int) and group < 2:
                return x1[:, half(group) * TPG:(half(group) + 1) * TPG, :]
            return x_tok[:]

        def norm_place(n, group):
            return LN.index("o") if (n, group) == ("x", 1) else LN.index(n)

        def x_turned(group):
            return (f_hi[:, 1], f_lo[:, 1]) if group == 1 else (act_hi[:], act_lo[:])

        def by_vector(n, group):
            return isinstance(group, int) and (group == 0 or (n, group) == ("x", 1))

        def norm_source(n, t, group):
            if n == "o":
                return att[:, FILLS["out"][t // 2], (t % 2) * C:(t % 2 + 1) * C]
            return (raw_x(group) if n == "x" else x1[:, half(group) * TPG:(half(group) + 1) * TPG, :])[:, t, :]

        def norm_signal(instruction, n, t):
            if n == "o" and t % 2:
                instruction.then_inc(reader_of("out", t // 2), 1)
            if n != "o" and t == TPG - 1:
                instruction.then_inc(signal[f"ln_{n}_norm"], 1)

        def tokens(dram, group):
            return dram[bass.ds(value(lambda g: g * GT, group), GT), :].rearrange("(t p) c -> p t c", p=P)

        block = ctx.enter_context(nc.Block())

        @block.sync
        def _(sp):
            def half_of(group):
                return slice(half(group) * TPG, (half(group) + 1) * TPG)

            def load_residual(group):
                sp.wait_ge(stored[half(group)], value(lambda g: 16 * (g // 2), group))
                stand_alone(sp)
                sp.dma_start(x1[:, half_of(group), :], tokens(x, group)).then_inc(
                    res_in[half(group)], 16)

            def spread_rows(group):
                read(sp, "gT", 0, group)
                stand_alone(sp)
                wait(sp, g_all_done, value(lambda g: g * E, group))
                for r in range(E // EG):
                    sp.dma_start(g_rows[32 * r:32 * r + 1, :, :], g_chan[EG * r:EG * (r + 1), :]).then_inc(
                        g_rows_in, 16)

            def store(group):
                sp.wait_ge(down_read, credited(2, 1, group))
                stand_alone(sp)
                sp.dma_start(tokens(out, group), x1[:, half_of(group), :]).then_inc(
                    stored[half(group)], 16)

            sp.dma_start(mask_c[:], masks).then_inc(mask_in, 16)
            sp.dma_start(col_c[:], columns).then_inc(columns_in, 16)
            for c in range(NWC):
                if c == 3:
                    sp.dma_start(row_c[:], rows.partition_broadcast(P)).then_inc(rows_in, 16)
                if c >= STAGE:
                    last = c - STAGE
                    sp.wait_ge(w_lo_done[last % 2], last // 2 + 1)
                sp.dma_start(stage[c % STAGE], weights[:, c * WCHUNK:(c + 1) * WCHUNK]).then_inc(
                    w_in[c % STAGE], 16)
            weights_split(sp, NWC)
            with sp.Fori(0, ITER) as i:
                spread_rows((i, 0))
                spread_rows((i, 1))
                store((i, 0))
                load_residual((i, 2))
                store((i, 1))
                load_residual((i, 3))
            spread_rows(GROUPS - 2)
            spread_rows(GROUPS - 1)
            store(GROUPS - 2)
            store(GROUPS - 1)
            for k in range(2):
                sp.wait_ge(stored[k], 16 * SEQS)

        @block.tensor
        def _(pe):
            def take(step, j, group):
                bank, n = fill(step, j, group)
                wait(pe, bank_read[bank], n - 1)
                return att[:, bank, :], bank_full[bank]

            def product(dst, w_at, w_n, a_hi, a_lo, tokens_stationary):
                n = 0
                for w, a in ((w_hi, a_hi), (w_lo, a_hi), (w_hi, a_lo)):
                    for k in range(KC):
                        wk = w[:, w_at(k):w_at(k) + w_n]
                        lhs, rhs = (a(k), wk) if tokens_stationary else (wk, a(k))
                        mm = pe.matmul(dst, lhs, rhs, start=n == 0, stop=n == 3 * KC - 1)
                        n += 1
                return mm

            def turn(step, source, group):
                for c in range(KC):
                    dst, full = take(step, c, group)
                    for t in range(TPG):
                        mm = pe.transpose(dst[:, t * P:(t + 1) * P], source[:, t, c * P:(c + 1) * P], ident)
                    mm.then_inc(full, 1)

            def turn_back(step, j, source, at, group):
                dst, full = take(step, j, group)
                for t in range(2):
                    for c in range(KC):
                        mm = pe.transpose(dst[:, t * C + c * P:t * C + (c + 1) * P],
                                          source[:, c, at + t * P:at + (t + 1) * P], ident)
                mm.then_inc(full, 1)

            def x_turn(group):
                after(pe, "ln_x_norm", group)
                turn("xT", x_tok, group)

            def k_project(group):
                for c in range(KC):
                    read(pe, "xT", c, group)
                for c in range(KC):
                    dst, full = take("k", c, group)
                    hi, lo = x_turned(group)
                    product(dst, lambda k: QKV0 + k * 3 * C + 2 * C + c * P, P,
                            lambda k: hi[:, k, :], lambda k: lo[:, k, :], False).then_inc(full, 1)

            def tile_product(dst, w_at, w_n, hi, lo, t):
                cols = slice(t * P, (t + 1) * P)
                return product(dst, w_at, w_n, lambda k: hi[:, k, cols], lambda k: lo[:, k, cols], True)

            def project(step, w_at, w_n):
                def run(group):
                    if step == "wo":
                        hi, lo = act_hi[:], act_lo[:]
                        after(pe, "oT_lo", group)
                    else:
                        hi, lo = x_turned(group)
                    for j in range(2):
                        dst, full = take(step, j, group)
                        for t in (2 * j, 2 * j + 1):
                            mm = tile_product(dst[:, (t % 2) * C:(t % 2 + 1) * C], w_at, w_n, hi, lo, t)
                        mm.then_inc(full, 1)
                return run

            def q_turn(group):
                after(pe, "softmax_mul", group)
                turn("qT", q_tok, group)

            def e_turn(i):
                def run(group):
                    after(pe, "k_exp", group)
                    turn_back(f"eT{i}", 0, k_chan, 2 * i * P, group)
                return run

            def state_sum(i):
                def run(group):
                    read(pe, f"eT{i}", 0, group)
                    if i == 0:
                        assert set(FILLS["st3"]) == set(FILLS["v"])
                        for c in range(KC):
                            take("st3", c, group)
                    for t in range(2):
                        for c in range(KC):
                            n = 2 * i + t
                            mm = pe.matmul(att[:, FILLS["st3"][c], 0:P],
                                           n_tok[:, 2 * (i % 2) + t, c * P:(c + 1) * P],
                                           v_tok[:, n, c * P:(c + 1) * P], start=n == 0, stop=n == TPS - 1)
                            if n == TPS - 1:
                                mm.then_inc(bank_full[FILLS["st3"][c]], 1)
                    if i < 2:
                        mm.then_inc(signal["st_part"], 1)
                return run

            def attend(group):
                seq_start = shift(group, -half(group))
                for c in range(KC):
                    read(pe, "st3", c, seq_start)
                if FILLS["qT"][1] != FILLS["out"][0]:
                    read(pe, "qT", 1, group)
                g = half(group)
                for j in range(2):
                    dst, full = take("out", j, group)
                    for t in (2 * j, 2 * j + 1):
                        for c in range(KC):
                            at = g * GT + t * P
                            mm = pe.matmul(dst[:, (t % 2) * C + c * P:(t % 2) * C + (c + 1) * P],
                                           q_chan[:, c, at:at + P], state[:, c, :], start=True, stop=True)
                    mm.then_inc(full, 1)

            def o_turn(group):
                for j in range(2):
                    read(pe, "out", j, group)
                turn("oT", n_tok, group)

            def f_turn(group):
                after(pe, "ln_f_norm", group)
                turn("fT", n_tok, group)

            def gate(group):
                for c in range(KC):
                    read(pe, "fT", c, group)
                pe.wait_ge(gate_parts_done, 2)
                dst, full = take("gate", 0, group)
                g = half(group)
                for t in range(TPG):
                    parts = [(part, k) for part in (f_hi, f_lo) for k in range(KC)]
                    for n, (part, k) in enumerate(parts):
                        mm = pe.matmul(dst[:, t * 2 * E:(t + 1) * 2 * E], part[:, g, k, t * P:(t + 1) * P],
                                       gate_parts[:, k].rearrange("p n e -> p (n e)"),
                                       start=n == 0, stop=n == len(parts) - 1)
                mm.then_inc(full, 1)

            def g_turn(group):
                after(pe, "route_weight", group)
                dst, full = take("gT", 0, group)
                for t in range(TPG):
                    mm = pe.transpose(dst[0:E, t * P:(t + 1) * P], r_root[:, 3, t, :], ident)
                mm.then_inc(full, 1)

            def warm(n):
                for _ in range(n):
                    pe.transpose(hid[:, 0, 0:P], ident, ident)

            mine = {
                "warm": warm, "xT": x_turn, "k": k_project, "q": project("q", lambda k: QKV0 + k * 3 * C, C),
                "v": project("v", lambda k: QKV0 + k * 3 * C + C, C), "qT": q_turn,
                "eT0": e_turn(0), "eT1": e_turn(1), "eT2": e_turn(2), "eT3": e_turn(3),
                "st0": state_sum(0), "st1": state_sum(1), "st2": state_sum(2), "st3": state_sum(3),
                "out": attend, "oT": o_turn, "wo": project("wo", lambda k: WO0 + k * C, C),
                "fT": f_turn, "gate": gate, "gT": g_turn,
                "w_ready": lambda n: weights_split(pe, n),
            }

            def up(j, group):
                g = half(group)
                if j == 0:
                    for c in range(KC):
                        read(pe, "fT", c, group)
                pe.wait_ge(y_rooted, credited(CH, j - 2, group))
                product(hid[:, j % 2, :], lambda k: UP0 + j * C + k * P, P,
                        lambda k: f_hi[:, g, k, :], lambda k: f_lo[:, g, k, :], False).then_inc(hid_done, 1)

            def down_product(j, group):
                at = DOWN0 + j * C
                pe.wait_ge(y_hi_done, counted(CH, j, group))
                for n, (w, part) in enumerate(((w_hi, y_hi), (w_lo, y_hi), (w_hi, y_lo))):
                    if n == 2:
                        pe.wait_ge(y_lo_done, credited(CH, j, group))
                    for t in range(TPG):
                        if j == 0 and n == 0 and t % 2 == 0:
                            pe.wait_ge(down_read, credited(2, t // 2 - 2, group))
                        mm = pe.matmul(down[:, t // 2, (t % 2) * C:(t % 2 + 1) * C],
                                       part[:, j % HB, t * P:(t + 1) * P], w[:, at:at + C],
                                       start=j == 0 and n == 0 and t % 2 == 0, stop=j == CH - 1 and n == 2,
                                       skip_group_check=True)
                mm.then_inc(y_used, 1)

            def sequence(i, slots):
                for s in range(2 * CH + LAG):
                    if s < 2 * CH:
                        up(*chunk(s, i))
                    if s >= LAG:
                        down_product(*chunk(s - LAG, i))
                    steps_at(slots, s, i, mine)

            pe.sem_inc(y_used, CH)
            pe.wait_ge(mask_in, 16)
            for name, g in PROLOGUE:
                if name in mine:
                    mine[name](g)
            weights_split(pe, NWC)
            with pe.Fori(0, ITER) as i:
                sequence(i, SLOTS)
            sequence(ITER, without_next(SLOTS))

        @block.scalar
        def _(act):
            def load_x(group):
                bank, n = fill("xT", KC - 1, shift(group, -1))
                act.wait_ge(bank_full[bank], n)
                act.dma_start(x_tok[:], tokens(x, group)).then_inc(x_in, 16)

            def ln_apply(n):
                def run(group):
                    if by_vector(n, group):
                        return
                    k = norm_place(n, group)
                    after(act, f"ln_{n}_apply", group)
                    for t in range(TPG):
                        norm_signal(nc.scalar.activation((x_tok if n == "x" else n_tok)[:, t, :],
                                                         norm_source(n, t, group), ACT.Identity,
                                                         scale=root[:, k, 2, t:t + 1],
                                                         bias=root[:, k, 0, t:t + 1]), n, t)
                return run

            def ln_root(n):
                def run(group):
                    step, k = f"ln_{n}_root", norm_place(n, group)
                    after(act, f"ln_{n}_stats", group)
                    nc.scalar.activation(root[:, k, 0, :], root[:, k, 3, :], ACT.Ln).then_inc(signal[step], 1)
                    after(act, step, group, 1)
                    nc.scalar.activation(root[:, k, 1, :], root[:, k, 0, :], ACT.Exp, scale=-0.5).then_inc(
                        signal[step], 1)
                return run

            def x_hi(group):
                if group != 1:
                    all_used(act, PROJECTIONS, "xT", group)
                for c in range(KC):
                    src = filled(act, "xT", c, group)
                    nc.scalar.activation(x_turned(group)[0][:, c, :], src, ACT.Copy).then_inc(signal["xT_hi"], 1)

            def k_out(group):
                all_used(act, ("eT3",), "k", group)
                g = half(group)
                for c in range(KC):
                    src = filled(act, "k", c, group)
                    nc.scalar.activation(k_chan[:, c, g * GT:(g + 1) * GT], src, ACT.Identity,
                                         bias=b_k[:, c:c + 1]).then_inc(reader_of("k", c), 1)

            def q_exponent(group):
                after(act, "softmax_sub", group)
                nc.scalar.activation(q_tok[:], q_tok[:], ACT.Exp).then_inc(signal["softmax_exp"], 1)

            def q_out(group):
                all_used(act, ("out",), "qT", group)
                g = half(group)
                for c in range(KC):
                    src = filled(act, "qT", c, group)
                    nc.scalar.activation(q_chan[:, c, g * GT:(g + 1) * GT], src, ACT.Copy).then_inc(
                        reader_of("qT", c), 1)

            def k_exponent(group):
                after(act, "k_max", group)
                for c in range(KC):
                    nc.scalar.activation(k_chan[:, c, :], k_chan[:, c, :], ACT.Exp, bias=kneg[:, 1, c:c + 1],
                                         accum_out=ksum[:, 0, c:c + 1]).then_inc(signal["k_exp"], 1)

            def e_out(i):
                def run(group):
                    if i == 0:
                        all_used(act, ("fT",), "eT0", group)
                    if i >= 2:
                        after(act, "st_part", group, i - 1)
                    src = filled(act, f"eT{i}", 0, group)
                    h = 2 * (i % 2)
                    nc.scalar.activation(n_tok[:, h:h + 2, :].rearrange("p t c -> p (t c)"), src,
                                         ACT.Copy).then_inc(reader_of(f"eT{i}", 0), 1)
                return run

            def o_scale(group):
                all_used(act, PROJECTIONS, "oT", group)
                for c in range(KC):
                    src = filled(act, "oT", c, group)
                    nc.scalar.activation(o_chan[:, c, :], src, ACT.Identity, bias=ln_b[:, c:c + 1],
                                         scale=ln_g[:, c:c + 1]).then_inc(reader_of("oT", c), 1)
                for c in range(KC):
                    read(act, "oT", c, group)
                    nc.scalar.activation(act_hi[:, c, :], o_chan[:, c, :], ACT.Copy).then_inc(signal["oT_hi"], 1)

            def f_split(group):
                wait(act, hid_done, value(lambda g: (g - 1) * CH, group))
                g = half(group)
                for c in range(KC):
                    src = filled(act, "fT", c, group)
                    nc.scalar.activation(f_hi[:, g, c, :], src, ACT.Copy).then_inc(signal["fT_hi"], 1)

            def gate_exp(group):
                read(act, "gate", 0, group)
                nc.scalar.activation(r_pick[:], r_score[:], ACT.Exp, scale=-1.0).then_inc(
                    signal["gate_exp"], 1)

            def route_root(group):
                after(act, "route_pick", group)
                nc.scalar.activation(r_root[:, 2, :, :], r_root[:, 1, :, :], ACT.Ln).then_inc(signal["route_root"], 1)
                after(act, "route_root", group, 1)
                nc.scalar.activation(r_root[:, 2, :, :], r_root[:, 2, :, :], ACT.Exp, scale=0.5).then_inc(
                    signal["route_root"], 1)

            def g_out(group):
                wait(act, g_rows_in, value(lambda g: g * 16 * (E // EG), group))
                src = filled(act, "gT", 0, group)
                nc.scalar.activation(g_chan[:], src[0:E, :], ACT.Copy).then_inc(reader_of("gT", 0), 1)

            def consts(_):
                act.wait_ge(columns_in, 16)
                nc.scalar.activation(gate_parts[:, :, 0, :], gate_w.rearrange("p (k e) -> p k e", e=E),
                                     ACT.Copy).then_inc(gate_parts_done, 1)

            mine = {
                "consts": consts,
                **{f"ln_{n}_root": ln_root(n) for n in LN}, **{f"ln_{n}_apply": ln_apply(n) for n in LN},
                "load_x": load_x, "xT": x_hi, "k": k_out, "softmax_exp": q_exponent,
                "qT": q_out, "k_exp": k_exponent, "eT0": e_out(0), "eT1": e_out(1), "eT2": e_out(2),
                "eT3": e_out(3), "oT": o_scale, "fT": f_split, "gate": gate_exp, "route_root": route_root,
                "gT": g_out,
            }

            def square(j, group):
                act.wait_ge(y_rooted, credited(CH, j, group))
                nc.scalar.activation(y[:, j % YB, :], y[:, j % YB, :], ACT.Square).then_inc(y_squared, 1)
                act.wait_ge(y_squared, counted(CH, j, group))
                act.wait_ge(y_used, credited(CH, j - HB, group))
                nc.scalar.activation(y_hi[:, j % HB, :], y[:, j % YB, :], ACT.Copy).then_inc(y_hi_done, 1)

            def sequence(i, slots):
                for s in range(2 * CH + LAG):
                    if s < 2 * CH:
                        square(*chunk(s, i))
                    steps_at(slots, s, i, mine)

            def split_weights(c):
                act.wait_ge(w_in[c % STAGE], 16 * (c // STAGE + 1))
                nc.scalar.activation(w_hi[:, c * WCHUNK:(c + 1) * WCHUNK], stage[c % STAGE],
                                     ACT.Copy).then_inc(w_hi_done, 1)

            mine["split"] = split_weights

            act.dma_start(x1[:, 0:TPG, :], tokens(x, 0)).then_inc(res_in[0], 16)
            act.dma_start(x1[:, TPG:TPS, :], tokens(x, 1)).then_inc(res_in[1], 16)
            nc.scalar.preload_act_table_set("natural_log_exp_and_others")
            act.sem_inc(down_read, 2)
            for name, g in PROLOGUE:
                if name in mine:
                    mine[name](g)
            with act.Fori(0, ITER) as i:
                sequence(i, SLOTS)
            sequence(ITER, without_next(SLOTS))

        @block.vector
        def _(dve):
            v = nc.vector

            class Run:

                def __init__(self, step, group):
                    self.step, self.group, self.n = step, group, 0

                def did(self, instruction):
                    instruction.then_inc(signal[self.step], 1)
                    self.n += 1

                def settle(self):
                    after(dve, self.step, self.group, self.n)

                def then(self, instruction):
                    self.did(instruction)
                    self.settle()

                def end(self):
                    assert self.n == SIGNALS[self.step], (self.step, self.n)

            def ln_stats(n):
                def run(group):
                    k, r, g = norm_place(n, group), Run(f"ln_{n}_stats", group), half(group)
                    if n == "x" and isinstance(group, int) and group < 2:
                        dve.wait_ge(res_in[group], 16)
                    elif n == "x":
                        dve.wait_ge(x_in, value(lambda q: 16 * (q - 1), group))
                    for t in range(TPG):
                        if n == "x":
                            src = raw_x(group)[:, t, :]
                        elif n == "o":
                            if t % 2 == 0:
                                bank = filled(dve, "out", t // 2, group)
                            src = bank[:, (t % 2) * C:(t % 2 + 1) * C]
                        else:
                            if t == 0:
                                for j in range(2):
                                    read(dve, "wo", j, group)
                            src = x1[:, g * TPG + t, :]
                        last = v.bn_stats(stats[:, k, t, :], src)
                    r.then(last)
                    stand_alone(dve)
                    for t in range(TPG):
                        last = v.bn_aggr(mv[:, k, t, :], stats[:, k, t, :])
                    r.then(last)
                    r.did(v.tensor_scalar(root[:, k, 3, :], mv[:, k, :, 1], EPS, None, ALU.add))
                    r.end()
                return run

            def ln_apply(n):
                def run(group):
                    k, r, g = norm_place(n, group), Run(f"ln_{n}_apply", group), half(group)
                    after(dve, f"ln_{n}_root", group)
                    r.then(v.tensor_tensor(root[:, k, 2, :], root[:, k, 1, :], root[:, k, 1, :], ALU.mult))
                    r.then(v.scalar_tensor_tensor(out=root[:, k, 2, :], in0=root[:, k, 2, :], scalar=-0.5,
                                                  in1=root[:, k, 3, :], op0=ALU.mult, op1=ALU.mult))
                    r.then(v.scalar_tensor_tensor(out=root[:, k, 2, :], in0=root[:, k, 2, :], scalar=1.5,
                                                  in1=root[:, k, 1, :], op0=ALU.add, op1=ALU.mult))
                    r.did(v.scalar_tensor_tensor(out=root[:, k, 0, :], in0=mv[:, k, :, 0], scalar=-1.0,
                                                 in1=root[:, k, 2, :], op0=ALU.mult, op1=ALU.mult))
                    r.end()
                    if by_vector(n, group):
                        if (n, group) == ("x", 1):
                            all_used(dve, ("xT",), "ln_x_apply", group)
                        for t in range(TPG):
                            norm_signal(v.tensor_scalar((x_tok if n == "x" else n_tok)[:, t, :],
                                                        norm_source(n, t, group), mv[:, k, t, 0:1],
                                                        root[:, k, 2, t:t + 1], ALU.subtract, ALU.mult), n, t)
                return run

            def x_lo(group):
                hi, lo = x_turned(group)
                for c in range(KC):
                    after(dve, "xT_hi", group, c + 1)
                    v.tensor_tensor(lo[:, c, :], att[:, FILLS["xT"][c], :], hi[:, c, :].bitcast(F32),
                                    ALU.subtract).then_inc(reader_of("xT", c), 1)

            def k_top(group):
                r = Run("k_top", group)
                g = half(group)
                for c in range(KC):
                    read(dve, "k", c, group)
                    r.did(v.tensor_reduce(kmax[:, c, g:g + 1], k_chan[:, c, g * GT:(g + 1) * GT], AX.X, ALU.max))
                r.end()

            def bias_add(step, target, bias, last_user):
                def run(group):
                    all_used(dve, (last_user,), step, group)
                    at = half(group) * TPG if step == "v" else 0
                    for j in range(2):
                        src = filled(dve, step, j, group)
                        v.tensor_tensor(target[:, at + 2 * j:at + 2 * j + 2, :],
                                        src.rearrange("p (t c) -> p t c", c=C),
                                        bias.unsqueeze(1).broadcast_to([P, 2, C]), ALU.add).then_inc(
                            reader_of(step, j), 1)
                return run

            def softmax_max(group):
                r = Run("softmax_max", group)
                for j in range(2):
                    read(dve, "q", j, group)
                r.did(v.tensor_reduce(qmax[:], q_tok[:].rearrange("p t (h d) -> p (t h) d", d=HD), AX.X, ALU.max))
                r.end()

            def softmax_sum(group):
                r = Run("softmax_sum", group)
                after(dve, "softmax_exp", group)
                r.then(v.tensor_reduce(qsum[:, 0, :], q_tok[:].rearrange("p t (h d) -> p (t h) d", d=HD),
                                       AX.X, ALU.add))
                r.did(v.reciprocal(qsum[:, 1, :], qsum[:, 0, :]))
                r.end()

            def k_max(group):
                r = Run("k_max", group)
                after(dve, "k_top", shift(group, 1))
                r.then(v.tensor_tensor(kneg[:, 0, :], kmax[:, :, 0], kmax[:, :, 1], ALU.max))
                r.did(v.tensor_scalar(kneg[:, 1, :], kneg[:, 0, :], -1.0, None, ALU.mult))
                r.end()

            def k_sum(group):
                r = Run("k_sum", group)
                after(dve, "k_exp", group)
                r.did(v.reciprocal(ksum[:, 1, :], ksum[:, 0, :]))
                r.end()

            def state_out(group):
                all_used(dve, ("out",), "state", group)
                after(dve, "k_sum", group)
                for c in range(KC):
                    src = filled(dve, "st3", c, group)
                    v.scalar_tensor_tensor(out=state[:, c, :], in0=src[:, 0:P], scalar=ksum[:, 1, c:c + 1],
                                           in1=same_head, op0=ALU.mult, op1=ALU.mult).then_inc(
                        reader_of("st3", c), 1)

            def o_lo(group):
                r = Run("oT_lo", group)
                for c in range(KC):
                    after(dve, "oT_hi", group, c + 1)
                    r.did(v.tensor_tensor(act_lo[:, c, :], o_chan[:, c, :], act_hi[:, c, :].bitcast(F32),
                                          ALU.subtract))
                r.end()

            def residual_add(group):
                after(dve, "residual", group)
                for j in range(2):
                    src = filled(dve, "wo", j, group)
                    at = half(group) * TPG + 2 * j
                    part = x1[:, at:at + 2, :].rearrange("p t c -> p (t c)")
                    v.tensor_tensor(part, src, part, ALU.add).then_inc(reader_of("wo", j), 1)

            def f_lo_out(group):
                for c in range(KC):
                    after(dve, "fT_hi", group, c + 1)
                    v.tensor_tensor(f_lo[:, half(group), c, :], att[:, FILLS["fT"][c], :],
                                    f_hi[:, half(group), c, :].bitcast(F32), ALU.subtract).then_inc(
                        reader_of("fT", c), 1)

            def logits(group):
                r = Run("logits", group)
                src = filled(dve, "gate", 0, group)[:, 0:TPG * 2 * E].rearrange("p (t n e) -> p t n e", n=2, e=E)
                r.then(v.tensor_copy(r_score[:], src[:, :, 0, :]))
                v.tensor_tensor(r_score[:], r_score[:], src[:, :, 1, :], ALU.add).then_inc(
                    reader_of("gate", 0), 1)
                r.end()

            def route_group(group):
                r = Run("route_group", group)
                after(dve, "gate_exp", group)
                scores = r_list[:, :, 0:E]
                by_group = scores.rearrange("p t (g e) -> p t g e", e=EG)
                pairs = r_half[:].rearrange("p h (t g) e -> p h t g e", g=EG)
                r.then(v.tensor_scalar(r_pick[:], r_pick[:], 1.0, None, ALU.add))
                r.then(v.reciprocal(r_score[:], r_pick[:]))
                r.then(v.tensor_tensor(scores, r_score[:], b_e.unsqueeze(1).broadcast_to([P, TPG, E]), ALU.add))
                r.did(v.tensor_tensor(pairs[:, 0], by_group[:, :, :, 0::2], by_group[:, :, :, 1::2], ALU.max))
                r.then(v.tensor_tensor(pairs[:, 1], by_group[:, :, :, 0::2], by_group[:, :, :, 1::2], ALU.min))
                r.did(v.tensor_tensor(r_pair[:, :, 0:2], r_half[:, 0], r_half[:, 1], ALU.add))
                r.then(v.tensor_tensor(r_pair[:, :, 2], r_half[:, 0, :, 0], r_half[:, 0, :, 1], ALU.add))
                best = r_group[:, 0]
                r.then(v.tensor_reduce(best.rearrange("p t g -> p (t g)"), r_pair[:], AX.X, ALU.max))
                other = best.unsqueeze(2).broadcast_to([P, TPG, EG, EG])
                own = best.unsqueeze(3).broadcast_to([P, TPG, EG, EG])
                above = r_above[:].rearrange("p n (t g) o -> p n t g o", g=EG)
                r.did(v.tensor_tensor(above[:, 0], other, own, ALU.is_gt))
                r.then(v.tensor_tensor(above[:, 1], other, own, ALU.is_equal))
                flat_above = r_above[:].rearrange("p n (t g) o -> p n t (g o)", g=EG)
                r.then(v.tensor_tensor(flat_above[:, 1], flat_above[:, 1],
                                       earlier.unsqueeze(1).broadcast_to([P, TPG, EG * EG]), ALU.mult))
                r.then(v.tensor_tensor(r_above[:, 0], r_above[:, 0], r_above[:, 1], ALU.add))
                keep = r_group[:, 1]
                r.then(v.tensor_reduce(keep.rearrange("p t g -> p (t g)"), r_above[:, 0], AX.X, ALU.add))
                r.then(v.tensor_scalar(keep, keep, 1.5, None, ALU.is_lt))
                r.did(v.tensor_tensor(by_group, by_group, keep.unsqueeze(3).broadcast_to([P, TPG, EG, EG]),
                                      ALU.mult))
                r.end()

            def route_pick(group):
                r = Run("route_pick", group)
                after(dve, "route_group", group)
                stand_alone(dve)
                for t in range(TPG):
                    last = v.max(r_best[:, t, :], r_list[:, t, 0:E])
                r.then(last)
                r.then(v.memset(r_best[:, :, 4:8], NONE))
                stand_alone(dve)
                for t in range(TPG):
                    last = v.match_replace(r_left[:, t, :], r_best[:, t, :], r_list[:, t, :], -NONE)
                r.then(last)
                r.then(v.tensor_scalar(r_pick[:], r_left[:, :, 0:E], -NONE, None, ALU.is_equal))
                r.then(v.tensor_tensor(r_root[:, 0], r_score[:], r_pick[:], ALU.mult))
                r.then(v.tensor_reduce(r_sum[:, 0, :], r_root[:, 0], AX.X, ALU.add))
                r.then(v.tensor_scalar(r_sum[:, 0, :], r_sum[:, 0, :], 1e-20, None, ALU.add))
                r.then(v.reciprocal(r_sum[:, 1, :], r_sum[:, 0, :]))
                r.then(v.scalar_tensor_tensor(out=r_root[:, 0], in0=r_root[:, 0], scalar=2.5,
                                              in1=r_sum[:, 1, :].unsqueeze(2).broadcast_to([P, TPG, E]),
                                              op0=ALU.mult, op1=ALU.mult))
                r.did(v.tensor_scalar(r_root[:, 1], r_root[:, 0], 1e-18, None, ALU.max))
                r.end()

            def route_weight(group):
                r = Run("route_weight", group)
                after(dve, "route_root", group)
                r.then(v.reciprocal(r_root[:, 1], r_root[:, 2]))
                r.then(v.tensor_tensor(r_root[:, 1], r_root[:, 0], r_root[:, 1], ALU.mult))
                r.then(v.tensor_tensor(r_root[:, 1], r_root[:, 1], r_root[:, 2], ALU.add))
                r.did(v.scalar_tensor_tensor(out=r_root[:, 3], in0=r_root[:, 1], scalar=0.5, in1=r_pick[:],
                                             op0=ALU.mult, op1=ALU.mult))
                r.end()

            def ffn_add(group):
                dve.wait_ge(y_used, credited(CH, CH - 1, group))
                for j in range(2):
                    src = down[:, j, :]
                    at = half(group) * TPG + 2 * j
                    part = x1[:, at:at + 2, :].rearrange("p t c -> p (t c)")
                    v.tensor_tensor(part, src, part, ALU.add).then_inc(down_read, 1)

            def consts(_):
                dve.wait_ge(rows_in, 16)
                dve.wait_ge(columns_in, 16)
                dve.wait_ge(mask_in, 16)
                dve.wait_ge(gate_parts_done, 1)
                v.tensor_tensor(gate_parts[:, :, 1, :], gate_w.rearrange("p (k e) -> p k e", e=E),
                                gate_parts[:, :, 0, :].bitcast(F32), ALU.subtract).then_inc(gate_parts_done, 1)

            mine = {
                "consts": consts,
                **{f"ln_{n}_stats": ln_stats(n) for n in LN}, **{f"ln_{n}_apply": ln_apply(n) for n in LN},
                "xT": x_lo, "k": k_top, "q": bias_add("q", q_tok, b_qv[:, 0:C], "qT"),
                "v": bias_add("v", v_tok, b_qv[:, C:2 * C], "st3"),
                "softmax_max": softmax_max, "softmax_sum": softmax_sum, "k_max": k_max, "k_sum": k_sum,
                "state": state_out, "oT": o_lo, "wo": residual_add, "fT": f_lo_out,
                "gate": logits, "route_group": route_group, "route_pick": route_pick, "route_weight": route_weight,
                "ffn_out": ffn_add,
            }

            def weigh(j, group):
                dve.wait_ge(hid_done, counted(CH, j, group))
                last = j - YB if j >= YB else max(n for n in range(CH) if n % YB == j) - CH
                dve.wait_ge(y_lo_done, credited(CH, last, group))
                if j >= SH:
                    dve.wait_ge(g_all_done, counted(E, j - SH, group))
                    v.scalar_tensor_tensor(out=y[:, j % YB, :], in0=hid[:, j % 2, :], scalar=0.0,
                                           in1=g_all[:, (j - SH) % GB, :], op0=ALU.max,
                                           op1=ALU.mult).then_inc(y_rooted, 1)
                else:
                    v.tensor_scalar(y[:, j % YB, :], hid[:, j % 2, :], 0.0, None, ALU.max).then_inc(y_rooted, 1)

            def split(j, group):
                dve.wait_ge(y_hi_done, counted(CH, j, group))
                v.tensor_tensor(y_lo[:, j % HB, :], y[:, j % YB, :], y_hi[:, j % HB, :].bitcast(F32),
                                ALU.subtract).then_inc(y_lo_done, 1)

            def sequence(i, slots):
                for s in range(2 * CH + LAG):
                    if s < 2 * CH:
                        weigh(*chunk(s, i))
                    if 1 <= s <= 2 * CH:
                        split(*chunk(s - 1, i))
                    steps_at(slots, s, i, mine)

            def split_weights(c):
                if c % 2 == 0:
                    weights_lo(dve, v, c)

            mine["split"] = split_weights

            dve.sem_inc(y_rooted, CH)
            dve.sem_inc(y_lo_done, CH)
            v.memset(r_list[:, :, E:E + 4], NONE).then_inc(list_end, 1)
            dve.wait_ge(list_end, 1)
            for name, g in PROLOGUE:
                if name in mine:
                    mine[name](g)
            weights_split(dve, NWC)
            with dve.Fori(0, ITER) as i:
                sequence(i, SLOTS)
            sequence(ITER, without_next(SLOTS))

        @block.gpsimd
        def _(pool):
            def softmax_sub(group):
                after(pool, "softmax_max", group)
                heads = q_tok[:].rearrange("p t (h d) -> p (t h) d", d=HD)
                nc.gpsimd.tensor_tensor(heads, heads, qmax[:].unsqueeze(2).broadcast_to([P, TPG * HEADS, HD]),
                                        ALU.subtract).then_inc(signal["softmax_sub"], 1)
                after(pool, "softmax_sub", group)

            def softmax_mul(group):
                after(pool, "softmax_sum", group)
                heads = q_tok[:].rearrange("p t (h d) -> p (t h) d", d=HD)
                nc.gpsimd.tensor_tensor(heads, heads, qsum[:, 1, :].unsqueeze(2).broadcast_to([P, TPG * HEADS, HD]),
                                        ALU.mult).then_inc(signal["softmax_mul"], 1)
                after(pool, "softmax_mul", group)

            def residual(group):
                after(pool, "ln_x_norm", group)
                stand_alone(pool)
                pool.wait_ge(res_in[half(group)], value(lambda g: 16 * (g // 2 + 1), group))
                at = half(group) * TPG
                part = x1[:, at:at + TPG, :]
                nc.gpsimd.tensor_tensor(part, part, b_o.unsqueeze(1).broadcast_to([P, TPG, C]),
                                        ALU.add).then_inc(signal["residual"], 1)
                after(pool, "residual", group)

            def consts(_):
                pool.wait_ge(rows_in, 16)

            def split_weights(c):
                if c % 2 == 1:
                    weights_lo(pool, nc.gpsimd, c)
                    pool.wait_ge(w_lo_done[1], c // 2 + 1)

            mine = {"consts": consts, "split": split_weights, "softmax_sub": softmax_sub,
                    "softmax_mul": softmax_mul, "residual": residual}

            def broadcast(e, group):
                if e == 0:
                    pool.wait_ge(g_rows_in, value(lambda g: 16 * (E // EG) * (g + 1), group))
                pool.wait_ge(y_rooted, credited(CH, e - GB + SH if e >= GB else e - GB, group))
                stand_alone(pool)
                row = 32 * (e // EG)
                nc.gpsimd.partition_broadcast(g_all[:, e % GB, :], g_rows[row:row + 1, e % EG, :], P).then_inc(
                    g_all_done, 1)
                pool.wait_ge(g_all_done, counted(E, e, group))
                stand_alone(pool)

            def sequence(i, slots):
                for s in range(2 * CH + LAG):
                    if s < 2 * CH and s % CH >= SH:
                        j, group = chunk(s, i)
                        broadcast(j - SH, group)
                    steps_at(slots, s, i, mine)

            for name, g in PROLOGUE:
                if name in mine:
                    mine[name](g)
            with pool.Fori(0, ITER) as i:
                sequence(i, SLOTS)
            sequence(ITER, without_next(SLOTS))


def kernel(L0_attn_x, L0_attn_Wq, L0_attn_bq, L0_attn_Wk, L0_attn_bk, L0_attn_Wv, L0_attn_bv, L0_attn_Wo,
           L0_attn_bo, L0_attn_ln_g, L0_attn_ln_b, L0_ffn_gate_w, L0_ffn_bias_e, L0_ffn_up_w, L0_ffn_down_w,
           L0_ffn_shared_up, L0_ffn_shared_down):
    import numpy as np
    import concourse.bacc as bacc
    from concourse.bass_utils import run_bass_kernel_spmd

    B, N, C = L0_attn_x.shape
    halves = C // P

    def by_channel(w):
        return np.asarray(w).T.reshape(halves, P, -1).transpose(1, 0, 2)

    qvk = np.concatenate([by_channel(L0_attn_Wq), by_channel(L0_attn_Wv), by_channel(L0_attn_Wk)], axis=2)
    ups = np.concatenate([np.asarray(L0_ffn_shared_up), np.asarray(L0_ffn_up_w).reshape(-1, C)], axis=0)
    chunks = ups.shape[0] // P
    ups = ups.reshape(chunks, P, halves, P).transpose(3, 0, 2, 1)
    downs = np.concatenate([np.asarray(L0_ffn_shared_down).reshape(C, -1, P).transpose(1, 0, 2),
                            np.asarray(L0_ffn_down_w)], axis=0)
    downs = downs.transpose(2, 0, 1)
    weights = np.concatenate([a.reshape(P, -1) for a in (qvk, by_channel(L0_attn_Wo), ups, downs)], axis=1)
    rows = np.concatenate([np.asarray(a) for a in (L0_attn_bq, L0_attn_bv, L0_attn_bo, L0_ffn_bias_e)])
    columns = np.concatenate([np.asarray(a).reshape(halves, P).T for a in (L0_attn_bk, L0_attn_ln_g, L0_attn_ln_b)]
                             + [by_channel(L0_ffn_gate_w).reshape(P, -1)], axis=1)
    head = np.arange(P) // 16
    earlier = (np.arange(4)[None, :] < np.arange(4)[:, None]).reshape(1, -1).repeat(P, axis=0)
    masks = np.concatenate([np.eye(P), head[:, None] == head[None, :], earlier], axis=1).astype(np.float32)

    arrays = {"x": np.asarray(L0_attn_x).reshape(B * N, C), "weights": weights, "rows": rows,
              "columns": columns, "masks": masks}
    arrays = {k: np.ascontiguousarray(a) for k, a in arrays.items()}
    nc = bacc.Bacc("TRN2", target_bir_lowering=False, num_devices=1)
    ins = [nc.dram_tensor(k, a.shape, F32, kind="ExternalInput").ap() for k, a in arrays.items()]
    out = nc.dram_tensor("out", (B * N, C), F32, kind="ExternalOutput").ap()
    layer_kernel(nc, *ins, out)
    result = run_bass_kernel_spmd(nc, [arrays], core_ids=[0])
    return result.results[0]["out"].reshape(B, N, C)
```
